# Optimizing a Trainium2 kernel written in Bass

```python
import numpy as np
import jax
import jax.numpy as jnp

def _softmax(x, axis=-1):
    return jax.nn.softmax(x, axis=axis)
def _gelu(x):
    return jax.nn.gelu(x, approximate=True)
def _silu(x):
    return jax.nn.silu(x)
def _sigmoid(x):
    return jax.nn.sigmoid(x)
def _layernorm(x, axis=-1, eps=1e-5):
    m = jnp.mean(x, axis=axis, keepdims=True)
    v = jnp.var(x, axis=axis, keepdims=True)
    return (x - m) / jnp.sqrt(v + eps)
def _scatter_add(tgt, idx, src, axis=0):
    return tgt.at[idx].add(src)
def _segment_sum(src, seg, n):
    return jax.ops.segment_sum(src, seg, n)

kernel_name = 'mk_conv_preact_d2_conv_nhwc384_65f3d7'

def setup_inputs(seed: int = 0):
    np.random.seed(seed)
    _w = jnp.asarray
    def _rec_inputs():
        import jax
        import jax.numpy as jnp
        _gk = jax.random.key(seed)
        x = -0.0004039 + 1 * jax.random.normal(jax.random.fold_in(_gk, 1), (8, 64, 64, 384), jnp.float32)
        return x
    x = _rec_inputs()
    def _L0_conv_setup():
        import jax, jax.numpy as jnp
        import numpy as np
        D_MODEL = 384
        D_STATE = 16
        D_CONV = 3
        EXPAND = 2
        D_INNER = EXPAND * D_MODEL
        HEADDIM = 64
        NHEADS = D_INNER // HEADDIM
        NGROUPS = 1
        CHUNK = 64
        D_IN_PROJ = 2 * D_INNER + 2 * NGROUPS * D_STATE + NHEADS
        CONV_DIM = D_INNER + 2 * NGROUPS * D_STATE

        def segsum(x):
            T = x.shape[-1]
            xe = jnp.broadcast_to(x[..., None], x.shape + (T,))
            mask_strict = jnp.tril(jnp.ones((T, T), bool), -1)
            xe = jnp.where(mask_strict, xe, 0.0)
            x_segsum = jnp.cumsum(xe, axis=-2)
            mask_incl = jnp.tril(jnp.ones((T, T), bool), 0)
            return jnp.where(mask_incl, x_segsum, -jnp.inf)

        def ssd_minimal_discrete(X, A, Bm, Cm, block_len):
            b, seqlen, h, p = X.shape
            c = seqlen // block_len
            X = X.reshape(b, c, block_len, h, p)
            Bm = Bm.reshape(b, c, block_len, h, -1)
            Cm = Cm.reshape(b, c, block_len, h, -1)
            A = A.reshape(b, c, block_len, h).transpose(0, 3, 1, 2)
            A_cumsum = jnp.cumsum(A, axis=-1)
            L = jnp.exp(segsum(A))
            Y_diag = jnp.einsum('bclhn,bcshn,bhcls,bcshp->bclhp', Cm, Bm, L, X)
            decay_states = jnp.exp(A_cumsum[:, :, :, -1:] - A_cumsum)
            states = jnp.einsum('bclhn,bhcl,bclhp->bchpn', Bm, decay_states, X)
            init = jnp.zeros_like(states[:, :1])
            states = jnp.concatenate([init, states], axis=1)
            A_last = jnp.pad(A_cumsum[:, :, :, -1], ((0, 0), (0, 0), (1, 0)))
            decay_chunk = jnp.exp(segsum(A_last))
            new_states = jnp.einsum('bhzc,bchpn->bzhpn', decay_chunk, states)
            states, final_state = (new_states[:, :-1], new_states[:, -1])
            state_decay_out = jnp.exp(A_cumsum)
            Y_off = jnp.einsum('bclhn,bchpn,bhcl->bclhp', Cm, states, state_decay_out)
            Y = (Y_diag + Y_off).reshape(b, seqlen, h, p)
            return (Y, final_state)
        key = jax.random.key(seed)
        ks = jax.random.split(key, 10)
        x = jax.random.normal(ks[0], (8, 64, 64, D_MODEL), jnp.float32)
        W_in = jax.random.normal(ks[1], (D_MODEL, D_IN_PROJ), jnp.float32) * 0.02
        W_conv = jax.random.normal(ks[2], (D_CONV, D_CONV, 1, CONV_DIM), jnp.float32) * 0.1
        b_conv = jax.random.normal(ks[3], (CONV_DIM,), jnp.float32) * 0.01
        dt = jnp.exp(jax.random.uniform(ks[4], (NHEADS,)) * (np.log(0.1) - np.log(0.001)) + np.log(0.001))
        dt = jnp.clip(dt, 0.0001, None)
        dt_bias = dt + jnp.log(-jnp.expm1(-dt))
        A_log = jnp.log(jax.random.uniform(ks[5], (NHEADS,), minval=1.0, maxval=16.0))
        D_param = jnp.ones((NHEADS,), jnp.float32)
        gamma = jnp.ones((D_INNER,), jnp.float32)
        beta = jnp.zeros((D_INNER,), jnp.float32)
        W_out = jax.random.normal(ks[6], (D_INNER, D_MODEL), jnp.float32) * 0.02
        return {'x': x, 'W_in': W_in, 'W_conv': W_conv, 'b_conv': b_conv, 'dt_bias': dt_bias, 'A_log': A_log, 'D_param': D_param, 'gamma': gamma, 'beta': beta, 'W_out': W_out}
    _L0_conv_all = _L0_conv_setup()
    _L0_conv_in = {k: v for k, v in _L0_conv_all.items() if k in ('W_in', 'W_conv', 'b_conv', 'dt_bias', 'A_log', 'D_param', 'gamma', 'beta', 'W_out', )}
    del _L0_conv_all

    def _L1_conv_setup():
        import jax, jax.numpy as jnp
        import numpy as np
        WINDOW = (1, 5, 20)
        FILL = 1.0

        def box_sum(x, axis, w):
            if w == 1:
                return x
            lo = w // 2
            hi = w - lo - 1
            xm = jnp.moveaxis(x, axis, -1)
            shp = xm.shape
            xr = xm.reshape(-1, 1, shp[-1])
            k = jnp.ones((1, 1, w), x.dtype)
            y = jax.lax.conv_general_dilated(xr, k, window_strides=(1,), padding=[(lo, hi)])
            return jnp.moveaxis(y.reshape(shp), -1, axis)
        key = jax.random.key(seed)
        x = jax.random.normal(key, (2, 256, 256, 384), dtype=jnp.float32)
        return {'x': x}
    _L1_conv_all = _L1_conv_setup()
    _L1_conv_in = {k: v for k, v in _L1_conv_all.items() if k in ()}
    del _L1_conv_all

    return {
        "x": x,
        "L0_conv_W_in": _L0_conv_in["W_in"],
        "L0_conv_W_conv": _L0_conv_in["W_conv"],
        "L0_conv_b_conv": _L0_conv_in["b_conv"],
        "L0_conv_dt_bias": _L0_conv_in["dt_bias"],
        "L0_conv_A_log": _L0_conv_in["A_log"],
        "L0_conv_D_param": _L0_conv_in["D_param"],
        "L0_conv_gamma": _L0_conv_in["gamma"],
        "L0_conv_beta": _L0_conv_in["beta"],
        "L0_conv_W_out": _L0_conv_in["W_out"],
    }

def reference(x, L0_conv_W_in, L0_conv_W_conv, L0_conv_b_conv, L0_conv_dt_bias, L0_conv_A_log, L0_conv_D_param, L0_conv_gamma, L0_conv_beta, L0_conv_W_out):
    import jax
    import jax.numpy as jnp
    def _L0_conv_ref(x, W_in, W_conv, b_conv, dt_bias, A_log, D_param, gamma, beta, W_out):
        import jax, jax.numpy as jnp
        import numpy as np
        D_MODEL = 384
        D_STATE = 16
        D_CONV = 3
        EXPAND = 2
        D_INNER = EXPAND * D_MODEL
        HEADDIM = 64
        NHEADS = D_INNER // HEADDIM
        NGROUPS = 1
        CHUNK = 64
        D_IN_PROJ = 2 * D_INNER + 2 * NGROUPS * D_STATE + NHEADS
        CONV_DIM = D_INNER + 2 * NGROUPS * D_STATE

        def segsum(x):
            T = x.shape[-1]
            xe = jnp.broadcast_to(x[..., None], x.shape + (T,))
            mask_strict = jnp.tril(jnp.ones((T, T), bool), -1)
            xe = jnp.where(mask_strict, xe, 0.0)
            x_segsum = jnp.cumsum(xe, axis=-2)
            mask_incl = jnp.tril(jnp.ones((T, T), bool), 0)
            return jnp.where(mask_incl, x_segsum, -jnp.inf)

        def ssd_minimal_discrete(X, A, Bm, Cm, block_len):
            b, seqlen, h, p = X.shape
            c = seqlen // block_len
            X = X.reshape(b, c, block_len, h, p)
            Bm = Bm.reshape(b, c, block_len, h, -1)
            Cm = Cm.reshape(b, c, block_len, h, -1)
            A = A.reshape(b, c, block_len, h).transpose(0, 3, 1, 2)
            A_cumsum = jnp.cumsum(A, axis=-1)
            L = jnp.exp(segsum(A))
            Y_diag = jnp.einsum('bclhn,bcshn,bhcls,bcshp->bclhp', Cm, Bm, L, X)
            decay_states = jnp.exp(A_cumsum[:, :, :, -1:] - A_cumsum)
            states = jnp.einsum('bclhn,bhcl,bclhp->bchpn', Bm, decay_states, X)
            init = jnp.zeros_like(states[:, :1])
            states = jnp.concatenate([init, states], axis=1)
            A_last = jnp.pad(A_cumsum[:, :, :, -1], ((0, 0), (0, 0), (1, 0)))
            decay_chunk = jnp.exp(segsum(A_last))
            new_states = jnp.einsum('bhzc,bchpn->bzhpn', decay_chunk, states)
            states, final_state = (new_states[:, :-1], new_states[:, -1])
            state_decay_out = jnp.exp(A_cumsum)
            Y_off = jnp.einsum('bclhn,bchpn,bhcl->bclhp', Cm, states, state_decay_out)
            Y = (Y_diag + Y_off).reshape(b, seqlen, h, p)
            return (Y, final_state)
        Bsz, H, W, C = x.shape
        L = H * W
        xf = x.reshape(Bsz, L, C)
        zxbcdt = xf @ W_in
        z = zxbcdt[..., :D_INNER]
        xBC = zxbcdt[..., D_INNER:D_INNER + CONV_DIM]
        dt = jax.nn.softplus(zxbcdt[..., D_INNER + CONV_DIM:] + dt_bias)
        xBC = xBC.reshape(Bsz, H, W, CONV_DIM)
        xBC = jax.lax.conv_general_dilated(xBC, W_conv, window_strides=(1, 1), padding='SAME', dimension_numbers=('NHWC', 'HWIO', 'NHWC'), feature_group_count=CONV_DIM) + b_conv
        xBC = jax.nn.silu(xBC).reshape(Bsz, L, CONV_DIM)
        x_inner = xBC[..., :D_INNER].reshape(Bsz, L, NHEADS, HEADDIM)
        gn = NGROUPS * D_STATE
        B_state = xBC[..., D_INNER:D_INNER + gn].reshape(Bsz, L, NGROUPS, D_STATE)
        C_state = xBC[..., D_INNER + gn:].reshape(Bsz, L, NGROUPS, D_STATE)
        rep = NHEADS // NGROUPS
        B_state = jnp.broadcast_to(B_state[:, :, :, None, :], (Bsz, L, NGROUPS, rep, D_STATE)).reshape(Bsz, L, NHEADS, D_STATE)
        C_state = jnp.broadcast_to(C_state[:, :, :, None, :], (Bsz, L, NGROUPS, rep, D_STATE)).reshape(Bsz, L, NHEADS, D_STATE)
        A = -jnp.exp(A_log)
        y, _ = ssd_minimal_discrete(x_inner * dt[..., None], A[None, None, :] * dt, B_state, C_state, CHUNK)
        y = y + x_inner * D_param[None, None, :, None]
        y = y.reshape(Bsz, L, D_INNER)
        mu = jnp.mean(y, axis=-1, keepdims=True)
        var = jnp.mean((y - mu) ** 2, axis=-1, keepdims=True)
        y = (y - mu) * jax.lax.rsqrt(var + 1e-05) * gamma + beta
        y = y * jax.nn.silu(z)
        y = y @ W_out
        return y.reshape(Bsz, H, W, D_MODEL)

    def _L1_conv_ref(x):
        import jax, jax.numpy as jnp
        import numpy as np
        WINDOW = (1, 5, 20)
        FILL = 1.0

        def box_sum(x, axis, w):
            if w == 1:
                return x
            lo = w // 2
            hi = w - lo - 1
            xm = jnp.moveaxis(x, axis, -1)
            shp = xm.shape
            xr = xm.reshape(-1, 1, shp[-1])
            k = jnp.ones((1, 1, w), x.dtype)
            y = jax.lax.conv_general_dilated(xr, k, window_strides=(1,), padding=[(lo, hi)])
            return jnp.moveaxis(y.reshape(shp), -1, axis)
        w0, w1, w2 = WINDOW
        s = box_sum(box_sum(x, 1, w0), 2, w1)
        num = box_sum(s * s, 3, w2)
        d = box_sum(box_sum(box_sum(x * x, 1, w0), 2, w1), 3, w2)
        c0 = box_sum(jnp.ones((x.shape[1],), x.dtype), 0, w0)
        c1 = box_sum(jnp.ones((x.shape[2],), x.dtype), 0, w1)
        norm = c0[:, None] * c1[None, :]
        denum = d * norm[None, :, :, None]
        return jnp.nan_to_num(num / denum, nan=FILL)

    def _gn(v, G=32, eps=1e-5):
        B_, H_, W_, C_ = v.shape
        g = v.reshape(B_, H_, W_, G, C_ // G)
        m = jnp.mean(g, axis=(1, 2, 4), keepdims=True)
        s = jnp.var(g, axis=(1, 2, 4), keepdims=True)
        return ((g - m) / jnp.sqrt(s + eps)).reshape(v.shape)

    def _ln_c(v, eps=1e-6):
        m = jnp.mean(v, axis=-1, keepdims=True)
        s = jnp.var(v, axis=-1, keepdims=True)
        return (v - m) / jnp.sqrt(s + eps)

    def _ln_t(v, eps=1e-5):
        m = jnp.mean(v, axis=-1, keepdims=True)
        s = jnp.var(v, axis=-1, keepdims=True)
        return (v - m) / jnp.sqrt(s + eps)

    def _to_tokens(v):
        B_, H_, W_, C_ = v.shape
        return v.reshape(B_, H_ * W_, C_)
    def _from_tokens(t, like):
        return t.reshape(like.shape)

    x = x + _L0_conv_ref(_gn(x), L0_conv_W_in, L0_conv_W_conv, L0_conv_b_conv, L0_conv_dt_bias, L0_conv_A_log, L0_conv_D_param, L0_conv_gamma, L0_conv_beta, L0_conv_W_out)
    x = x + _L1_conv_ref(_gn(x))
    return x


_drawn_inputs = setup_inputs


def setup_inputs(seed=0):
    import zlib

    import numpy as np

    out = dict(_drawn_inputs(seed))
    spreads = {'L0_conv_D_param': (1.0, 0.6), 'L0_conv_gamma': (1.0, 0.6), 'L0_conv_beta': (0.0, 0.711)}
    factors = {'L0_conv_b_conv': 5.895, 'L0_conv_dt_bias': 8.0, 'L0_conv_A_log': 8.0}
    for name, (base, spread) in spreads.items():
        noise = np.random.default_rng([zlib.crc32(name.encode()), seed]).standard_normal(out[name].shape)
        drawn = base * np.exp(spread * noise) if base else spread * noise
        out[name] = jnp.asarray(drawn.astype(out[name].dtype))
    for name, factor in factors.items():
        out[name] = (out[name] * factor).astype(out[name].dtype)
    return out
```

```python
from contextlib import ExitStack

import numpy as np

import concourse.bass as bass
from concourse import mybir

F32 = mybir.dt.float32
ALU = mybir.AluOpType
ACT = mybir.ActivationFunctionType

P = 128
NB, H, W, C = 8, 64, 64, 384
KC = C // P
HEADS, HD, NS = 12, 64, 16
DI = HEADS * HD
ZC = DI // P
XC = ZC + 1
C_AT = 32
ROWS = 8
TT = ROWS * W
TILES = H // ROWS
SUBS = TT // P
NSUB = TILES * SUBS
HG = 4
NG = HEADS // HG
HB = DI // 2
TAPS = 9
PAIRS = (XC + 1) // 2
TPP = 2 * TAPS
TPT = PAIRS * TPP
SPT = XC + 1
GROUPS = 32
GC = C // GROUPS
WIN_W, WIN_C = 5, 20
HALF = TT // 2
EPS = 1e-5
LOG_TERMS = 8
NORMS = 2 * KC
SP_STEPS = 10 + LOG_TERMS
GN_STEPS = 10
START = 4
TINY = float(np.finfo(np.float32).tiny)
AHEAD = WIN_C - WIN_C // 2 - 1
BAND_LO = [0, P - AHEAD, 2 * P - AHEAD]
BAND_HI = [P + WIN_C // 2, 2 * P + WIN_C // 2, C]
BANDC = max(h - l for l, h in zip(BAND_LO, BAND_HI))
CONSTS = ["w_xbc", "w_z", "w_dt", "w_out", "w_conv", "b_conv", "chan", "dt_bias", "neg_a", "upto", "after", "ones",
          "ident", "to_group", "from_group", "band_w", "band_wn", "band_c"]
IN_PROJ = [(1, (2, 3)), (1, (4, 5)), (1, (6,)), (2, (0, 1))]


def at_(e, v):
    return v if isinstance(v, int) else e.snap(v)


def walk_scan(e, gb, slot):
    slot(0, 0, 0, first=True)
    with e.Fori(0, TILES // 2 - 1) as pair:
        t0 = e.snap(pair * 2)
        for k in range(1, 2 * SUBS + 1):
            slot(t0 + k // SUBS, (k // SUBS) % 2, k % SUBS)
    for k in range(1, 2 * SUBS):
        t = TILES - 2 + k // SUBS
        slot(t, t % 2, k % SUBS, left=TILES - 1 - t)


def walk_layer1(e, slot):
    for i in range(SUBS):
        slot(0, i, stages=min(i + 1, 3))
    with e.Fori(1, TILES - 1) as t:
        for i in range(SUBS):
            slot(t, i)
    for i in range(SUBS):
        slot(TILES - 1, i, last=True)


def build(nc, A):
    with ExitStack() as ctx:
        def sb(name, *shape):
            return ctx.enter_context(nc.sbuf_tensor(name, list(shape), F32))

        def sem(name):
            return ctx.enter_context(nc.semaphore(name))

        w_xbc = sb("w_xbc", P, KC, XC * P)
        w_z = sb("w_z", P, KC, DI)
        w_dt = sb("w_dt", P, KC, HEADS)
        w_out = sb("w_out", P, ZC, C)
        w_conv = sb("w_conv", P, XC, TAPS)
        b_conv = sb("b_conv", P, XC)
        chan = sb("chan", P, 3, ZC)
        dt_bias = sb("dt_bias", P, HEADS)
        neg_a = sb("neg_a", P, HEADS)
        upto = sb("upto", P, P)
        after = sb("after", P, P)
        ones = sb("ones", P, P)
        ident = sb("ident", P, P)
        to_group = sb("to_group", P, KC, GROUPS)
        from_group = sb("from_group", GROUPS, C)
        band_w = sb("band_w", P, P)
        band_wn = sb("band_wn", P, P)
        band_c = sb("band_c", P, KC, BANDC)
        diag_d = sb("diag_d", P, ZC, P)
        minus_half = sb("minus_half", P, KC)

        xb = sb("xb", P, KC, (H + 1) * W)
        stats = sb("stats", P, KC, 2 * TILES, 6)
        mean_var = sb("mean_var", P, KC, 2)
        g_mean = sb("g_mean", P, KC)
        g_tmp = sb("g_tmp", P, KC)
        g_var = sb("g_var", P, KC)
        g_rstd = sb("g_rstd", P, KC)
        g_red = sb("g_red", GROUPS, 2)
        dt = sb("dt", P, NSUB * HEADS)
        a_dt = sb("a_dt", P, NSUB * HEADS)
        e_from = sb("e_from", P, NSUB * HEADS)
        e_to = sb("e_to", P, NSUB * HEADS)
        e_all = sb("e_all", P, NSUB * HEADS)
        sp0, sp1, sp2 = (sb(f"softplus{n}", P, NSUB * HEADS) for n in range(3))

        cb = sb("cb", P, XC, ROWS + 2, W + 2)
        xs = sb("xs", P, 2, XC, TT)
        ct = sb("ct", NS, 2, TT)
        gate = sb("gate", P, 2, ZC, HALF)
        xres = sb("xres", P, 2, KC, HALF)

        a_tri = sb("a_tri", P, NG, HG * P)
        mix = sb("mix", P, NG, HG * P)
        bc_m = sb("bc_m", P, P)
        b_tok = sb("b_tok", P, 2, NS)
        x_dt = sb("x_dt", P, DI)
        x_end = sb("x_end", P, DI)
        y_in = sb("y_in", P, DI)
        y = sb("y", P, DI)
        state = sb("state", NS, DI)
        ln_st = sb("ln_st", P, 2, 6)
        ln_mv = sb("ln_mv", P, 2)
        ln_vm = sb("ln_vm", P, 2)
        ln_rs = sb("ln_rs", P, 2)
        aff = sb("aff", P, ZC, P)

        xg = a_tri[:, :, :]
        x1c = mix[:, :, :]
        out_b = gate[:].rearrange("p h c n -> p (h c n)")[:, 0:SUBS * C].rearrange("p (s c) -> p s c", s=SUBS)
        xs_flat = xs[:].rearrange("p u c n -> p (u c n)")

        def carve(n):
            return xs_flat[:, n * 2 * C:(n + 1) * 2 * C].rearrange("p (n c) -> p n c", n=2)

        xg_t, sq_t, s2, qw, l1w = (carve(n) for n in range(5))
        den, rec = l1w[:, 0], l1w[:, 1]
        base = carve(5)[:, 0]
        ratio = carve(5)[:, 1]

        pb = [ctx.enter_context(nc.psum_tensor(f"proj{i}", [P, 512], F32)) for i in range(2)]
        tr = ctx.enter_context(nc.psum_tensor("tr", [P, 2, 512], F32))
        ring = [ctx.enter_context(nc.psum_tensor(f"ring{i}", [P, 512], F32)) for i in range(2)]
        yp = ctx.enter_context(nc.psum_tensor("yp", [P, 2, 512], F32))


        def l1_num(i):
            return ring[0][:] if i % 2 == 0 else yp[:, 0]

        def l1_den(i):
            return ring[1][:] if i % 2 == 0 else yp[:, 1]

        s_const, s_setup = sem("consts_loaded"), sem("setup_done")
        s_half, s_expa = sem("minus_half_ready"), sem("exp_a_ready")
        s_x = sem("x_loaded")
        s_res = [sem(f"residual_loaded{h}") for h in range(2)]
        s_out = [sem(f"out_stored{i}") for i in range(SUBS)]
        s_xst = sem("x_stats")
        s_gp, s_gv, s_gr = sem("gn_summed"), sem("gn_step"), sem("gn_rstd")
        s_norm, s_zero = sem("x_normalised"), sem("image_zeroed")
        s_dtp, s_sp, s_dte, s_sum, s_exps = (
            sem(n) for n in ("dt_projected", "softplus_step", "dt_exp", "a_summed", "decays_ready"))
        s_r0p, s_r0 = sem("row0_projected"), sem("row0_stored")
        s_xbc, s_ev = sem("xbc_projected"), sem("xbc_stored")
        s_tap, s_silu = sem("conv_tap"), sem("silu_done")
        s_z, s_zev = sem("z_projected"), sem("z_stored")
        s_op, s_oev = sem("out_projected"), sem("out_added")
        s_x1st = sem("x1_stats")
        s_xt, s_xtr = sem("x_transposed"), sem("x_transposed_read")
        s_at, s_d, s_e, s_m = sem("a_tri_ready"), sem("decay_summed"), sem("decay_ready"), sem("mix_ready")
        s_y, s_yoff, s_t1 = sem("y_summed"), sem("y_of_state"), sem("y_of_state_read")
        s_xe, s_sn, s_ss, s_sa = sem("x_end_ready"), sem("state_product"), sem("state_scaled"), sem("state_added")
        s_yr, s_yst, s_var, s_rs, s_yn = sem("y_ready"), sem("y_stats"), sem("y_var"), sem("y_rstd"), sem("y_normed")
        s_ynt, s_aff, s_g = sem("y_transposed"), sem("y_scaled"), sem("gated")
        s_lx, s_lc = sem("l1_x_ready"), sem("l1_copy_ready")
        s_lt, s_la, s_lw, s_lb, s_lq = (
            sem(n) for n in ("l1_transposed", "l1_squares", "l1_box_w", "l1_box_read", "l1_box_c"))
        s_ls, s_lo = sem("l1_step"), sem("l1_out")

        block = ctx.enter_context(nc.Block())

        @block.sync
        def _(e):
            for counted in (*s_out,):
                e.sem_inc(counted, START)
            bufs = dict(w_xbc=w_xbc, w_z=w_z, w_dt=w_dt, w_out=w_out, w_conv=w_conv, b_conv=b_conv, chan=chan,
                        dt_bias=dt_bias, neg_a=neg_a, upto=upto, after=after, ones=ones, ident=ident,
                        to_group=to_group, from_group=from_group, band_w=band_w, band_wn=band_wn, band_c=band_c)
            for name in CONSTS:
                e.dma_start(bufs[name][:], A[name]).then_inc(s_const, 16)

            def load(g, t):
                at = t * TT if isinstance(t, int) else e.snap(t * TT)
                e.dma_start(xb[:, :, bass.ds(at, TT)], A["x"][bass.ds(g, 1)].rearrange("g p k n -> (g p) k n")
                            ).then_inc(s_x, 16)

            def image(gb, more):
                def slot(t, u, i, first=False, left=TILES):
                    g = at_(e, gb + t)
                    if i < 2:
                        e.wait_ge(s_xtr, START + g * SUBS + i + 1)
                        e.dma_start(xres[:, i], A["x"][bass.ds(g, 1), :, :, i * HALF:(i + 1) * HALF]
                                    .rearrange("g p k n -> (g p) k n")).then_inc(s_res[i], 16)

                walk_scan(e, gb, slot)
                with e.Fori(0, TILES) as t:
                    g = at_(e, gb + t)
                    if more:
                        e.wait_ge(s_lx, START + g + 1)
                        e.wait_ge(s_lc, START + g + 1)
                        load(e.snap(g + TILES), t)
                    for i in range(SUBS):
                        e.wait_ge(s_lo, START + g * SUBS + i + 1)
                        e.dma_start(A["out"][bass.ds(g, 1), i * P:(i + 1) * P].rearrange("g p c -> (g p) c"),
                                    out_b[:, i]).then_inc(s_out[i], 16)

            for t in range(TILES):
                load(t, t)
            if NB > 1:
                with e.Fori(0, NB - 1) as b:
                    image(e.snap(b * TILES), True)
            image((NB - 1) * TILES, False)
            for i in range(SUBS):
                e.wait_ge(s_out[i], START + 16 * NB * TILES)

        @block.gpsimd
        def _(e):
            for counted in (s_xe, s_rs):
                e.sem_inc(counted, START)
            e.memset(minus_half[:], -0.5).then_inc(s_half, 1)
            e.wait_ge(s_half, 1)

            def root(n):
                e.wait_ge(s_gv, n * GN_STEPS + GN_STEPS)
                e.tensor_tensor(g_rstd[:], g_var[:], minus_half[:], ALU.pow).then_inc(s_gr, 1)

            def ln_root(sp):
                e.wait_ge(s_var, sp + 1)
                e.wait_ge(s_yn, START + sp)
                e.tensor_tensor(ln_rs[:, 0:1], ln_vm[:, 0:1], minus_half[:, 0:1], ALU.pow).then_inc(s_rs, 1)
                e.wait_ge(s_rs, START + sp * 2 + 1)
                e.tensor_tensor(ln_rs[:, 1:2], ln_vm[:, 1:2], ln_rs[:, 0:1], ALU.mult).then_inc(s_rs, 1)

            with e.Fori(0, NB) as b:
                gb = e.snap(b * TILES)
                root(e.snap(b * 2))
                e.wait_ge(s_sp, (b + 1) * SP_STEPS)
                e.wait_ge(s_exps, b * 3 + 3)

                def slot(t, u, i, first=False, left=TILES):
                    s = e.snap((gb + t) * SUBS + i)
                    at = e.snap((t * SUBS + i) * HEADS) if not isinstance(t, int) else (t * SUBS + i) * HEADS
                    e.wait_ge(s_d, START + s * NG)
                    for j in range(NG):
                        a = a_dt[:, bass.ds(at + j * HG, HG)]
                        e.tensor_tensor(a_tri[:, j].rearrange("p (h l) -> p h l", h=HG),
                                        a.unsqueeze(2).to_broadcast([P, HG, P]),
                                        upto[:].unsqueeze(1).to_broadcast([P, HG, P]), ALU.mult).then_inc(s_at, 1)
                    if not first:
                        ln_root(e.snap(s - 1))
                    e.wait_ge(s_xtr, START + s + 1)
                    e.wait_ge(s_sn, START + s * 2)
                    e.tensor_tensor(x_end[:].rearrange("p (h d) -> p h d", h=HEADS),
                                    x_dt[:].rearrange("p (h d) -> p h d", h=HEADS),
                                    e_to[:, bass.ds(at, HEADS)].unsqueeze(2).to_broadcast([P, HEADS, HD]),
                                    ALU.mult).then_inc(s_xe, 1)
                    e.wait_ge(s_yoff, START + s * 2 + 2)
                    e.wait_ge(s_sa, START + s * 2)
                    sv = state[:].rearrange("p (h d) -> p h d", h=HEADS)
                    e.tensor_tensor(sv, sv, e_all[0:NS, bass.ds(at, HEADS)].unsqueeze(2).to_broadcast([NS, HEADS, HD]),
                                    ALU.mult).then_inc(s_ss, 1)

                walk_scan(e, gb, slot)
                ln_root(e.snap((gb + TILES) * SUBS - 1))
                root(e.snap(b * 2 + 1))

        @block.tensor
        def _(e):
            for counted in (s_d, s_sn, s_y, s_yoff, s_ynt, s_op, s_lq, s_lt):
                e.sem_inc(counted, START)
            def gn_sums(n):
                for r, ready in enumerate((3, 8)):
                    e.wait_ge(s_gv, n * GN_STEPS + ready)
                    for k in range(KC):
                        src = mean_var[:, k, 0:1] if r == 0 else g_tmp[:, k:k + 1]
                        mm = e.matmul(yp[0:GROUPS, 0, r:r + 1], to_group[:, k], src, start=(k == 0), stop=(k == KC - 1))
                    mm.then_inc(s_gp, 1)
                    e.wait_ge(s_gv, n * GN_STEPS + ready + 1)
                    for k in range(KC):
                        mm = e.matmul(yp[:, 1, KC * r + k:KC * r + k + 1], from_group[:, k * P:(k + 1) * P],
                                      g_red[:, r:r + 1], start=True, stop=True)
                    mm.then_inc(s_gp, 1)

            def in_proj(gx, tx, c):
                e.wait_ge(s_ev, START + (gx * XC + c) * 2)
                for k in range(KC):
                    mm = e.matmul(pb[0][:], w_xbc[:, k, c * P:(c + 1) * P], xb[:, k, bass.ds(tx * TT + W, TT)],
                                  start=(k == 0), stop=(k == KC - 1))
                mm.then_inc(s_xbc, 1)

            def z_proj(gx, tx, h, q, outs):
                e.wait_ge(s_zev, START + gx * 6 + h * 3 + q)
                e.wait_ge(s_oev, START + outs)
                for c in range(2):
                    for k in range(KC):
                        mm = e.matmul(pb[1][:, c * HALF:(c + 1) * HALF], w_z[:, k, (2 * q + c) * P:(2 * q + c + 1) * P],
                                      xb[:, k, bass.ds(tx * TT + h * HALF, HALF)], start=(k == 0), stop=(k == KC - 1))
                mm.then_inc(s_z, 1)

            def out_proj(gx, h, q, gated, zs):
                e.wait_ge(s_g, START + gated)
                e.wait_ge(s_zev, START + zs)
                e.wait_ge(s_oev, START + gx * 4 + h * 2 + q)
                for n, m in enumerate(((0, 1), (2,))[q]):
                    for k in range(ZC):
                        mm = e.matmul(pb[1][:, n * HALF:(n + 1) * HALF], w_out[:, k, m * P:(m + 1) * P], gate[:, h, k],
                                      start=(k == 0), stop=(k == ZC - 1))
                mm.then_inc(s_op, 1)

            def y_transpose(sp):
                e.wait_ge(s_yn, START + sp + 1)
                for c in range(ZC):
                    mm = e.transpose(tr[:, c // KC, (c % KC) * P:(c % KC + 1) * P], y[:, c * P:(c + 1) * P], ident[:])
                mm.then_inc(s_ynt, 1)

            e.wait_ge(s_const, 16 * len(CONSTS))
            with e.Fori(0, NB) as b:
                gb = e.snap(b * TILES)
                gn_sums(e.snap(b * 2))
                e.wait_ge(s_norm, b * NORMS + KC)
                e.wait_ge(s_zero, b + 1)
                for c in range(XC):
                    for k in range(KC):
                        mm = e.matmul(tr[:, 0, c * W:(c + 1) * W], w_xbc[:, k, c * P:(c + 1) * P], xb[:, k, 0:W],
                                      start=(k == 0), stop=(k == KC - 1))
                mm.then_inc(s_r0p, 1)
                for c in range(2):
                    in_proj(gb, 0, c)
                e.wait_ge(s_norm, (b + 1) * NORMS)
                for n in range(NSUB):
                    for k in range(KC):
                        mm = e.matmul(yp[:, 0, n * HEADS:(n + 1) * HEADS], xb[:, k, n * P:(n + 1) * P], w_dt[:, k],
                                      start=(k == 0), stop=(k == KC - 1))
                mm.then_inc(s_dtp, 1)
                for c in range(2, 4):
                    in_proj(gb, 0, c)
                e.wait_ge(s_sp, (b + 1) * SP_STEPS)
                for mask, bank in ((upto, yp[:, 0]), (after, yp[:, 1]), (ones, ring[0][:])):
                    e.matmul(bank[:, 0:NSUB * HEADS], mask[:], a_dt[:], start=True, stop=True).then_inc(s_sum, 1)
                for c in range(4, XC):
                    in_proj(gb, 0, c)
                for c in range(2):
                    in_proj(e.snap(gb + 1), 1, c)
                for q in range(3):
                    z_proj(gb, 0, 0, q, gb * 4)

                def slot(t, u, i, first=False, left=TILES):
                    g = at_(e, gb + t)
                    s = e.snap(g * SUBS + i)
                    tok = slice(i * P, (i + 1) * P)
                    off, chunks = IN_PROJ[i]
                    chunks = chunks if off <= left else ()
                    e.wait_ge(s_silu, (g + 1) * SPT)
                    e.wait_ge(s_xtr, START + s)
                    if first:
                        e.wait_ge(s_r0, b + 1)
                        e.wait_ge(s_exps, b * 3 + 3)
                    else:
                        e.wait_ge(s_aff, START + s - 1)
                    for c in range(ZC):
                        e.transpose(tr[:, c // KC, (c % KC) * P:(c % KC + 1) * P], xs[:, u, c, tok], ident[:])
                    e.transpose(tr[:, 1, HB:HB + NS], xs[0:NS, u, ZC, tok], ident[0:NS, 0:NS])
                    e.matmul(tr[:, 0, HB:HB + P], xs[0:NS, u, ZC, tok], ct[:, u, tok],
                             start=True, stop=True).then_inc(s_xt, 1)
                    if chunks:
                        in_proj(e.snap(g + off), e.snap(t + off), chunks[0])
                    if i == 1:
                        z_proj(g, t, 1, 0, g * 4)
                    if i == 3 and left:
                        z_proj(e.snap(g + 1), e.snap(t + 1), 0, 0, g * 4 + 2)
                    for j in range(NG):
                        if j == 0:
                            e.wait_ge(s_sa, START + s * 2)
                        if j == 2:
                            if not first:
                                e.wait_ge(s_xtr, START + s + 1)
                                y_transpose(e.snap(s - 1))
                            e.wait_ge(s_e, s * NG + 1)
                        e.wait_ge(s_at, s * NG + j + 1)
                        e.matmul(ring[j % 2][:], after[:], a_tri[:, j], start=True, stop=True).then_inc(s_d, 1)
                    if len(chunks) > 1:
                        in_proj(e.snap(g + off), e.snap(t + off), chunks[1])
                    e.wait_ge(s_yr, START + s)
                    e.wait_ge(s_xtr, START + s + 1)
                    for c in range(ZC):
                        e.matmul(yp[:, c // KC, (c % KC) * P:(c % KC + 1) * P], xs[:, u, c, tok], diag_d[:, c],
                                 start=(c % KC == 0), stop=False, skip_group_check=True)
                    for h in range(HEADS):
                        if h % HG == 0:
                            e.wait_ge(s_m, s * NG + h // HG + 1)
                        at = (h % (HEADS // 2)) * HD
                        mm = e.matmul(yp[:, h // (HEADS // 2), at:at + HD],
                                      mix[:, h // HG, (h % HG) * P:(h % HG + 1) * P],
                                      x_dt[:, h * HD:(h + 1) * HD], start=False,
                                      stop=(h % (HEADS // 2) == HEADS // 2 - 1), skip_group_check=True)
                    mm.then_inc(s_y, 1)
                    if first:
                        e.wait_ge(s_zero, b + 1)
                    for n in range(2):
                        e.wait_ge(s_e, s * NG + n + 2)
                        e.matmul(ring[1 - n][:, 0:HB], ct[:, u, tok], state[:, n * HB:(n + 1) * HB],
                                 start=True, stop=True).then_inc(s_yoff, 1)
                    if i == 1:
                        z_proj(g, t, 1, 1, g * 4)
                    if i == 3 and left:
                        z_proj(e.snap(g + 1), e.snap(t + 1), 0, 1, g * 4 + 2)
                    e.wait_ge(s_xe, START + s + 1)
                    for n in range(2):
                        e.wait_ge(s_t1, s * 2 + n + 1)
                        e.matmul(ring[1 - n][0:NS, 0:HB], b_tok[:, i % 2], x_end[:, n * HB:(n + 1) * HB],
                                 start=True, stop=True).then_inc(s_sn, 1)
                    if i == 1:
                        z_proj(g, t, 1, 2, g * 4)
                    if i == 3 and left:
                        z_proj(e.snap(g + 1), e.snap(t + 1), 0, 2, g * 4 + 2)
                    for q in range(2):
                        if i == 0 and not first:
                            out_proj(e.snap(g - 1), 1, q, s, g * 6 + 3)
                        if i == 2:
                            out_proj(g, 0, q, s, g * 6 + 6)

                walk_scan(e, gb, slot)
                end = e.snap(gb + TILES)
                y_transpose(e.snap(end * SUBS - 1))
                for q in range(2):
                    out_proj(e.snap(end - 1), 1, q, end * SUBS, end * 6)

                gn_sums(e.snap(b * 2 + 1))

                def l1_stage1(q, i):
                    g = e.snap(gb)
                    e.wait_ge(s_la, START + q * 2)
                    for k in range(KC):
                        mm = e.transpose(pb[0][:, k * P:(k + 1) * P], xg[:, k, i * P:(i + 1) * P], ident[:])
                    mm.then_inc(s_lt, 1)

                def l1_stage2(q, i):
                    e.wait_ge(s_la, START + q * 2 + 2)
                    e.wait_ge(s_lb, START + q * 2)
                    for src, band, n in ((xg_t, band_w, 0), (sq_t, band_wn, 1)):
                        for k in range(KC):
                            mm = e.matmul(tr[:, n, k * P:(k + 1) * P], src[:, i % 2, k * P:(k + 1) * P], band[:],
                                          start=True, stop=True)
                    mm.then_inc(s_lw, 1)

                def l1_stage3(q, i):
                    e.wait_ge(s_lb, START + q * 2 + 2)
                    e.wait_ge(s_lo, START + q - 1)
                    for src, bank in ((qw, l1_den(i)), (s2, l1_num(i))):
                        for k in range(KC):
                            mm = e.matmul(bank[:, BAND_LO[k]:BAND_HI[k]], src[:, i % 2, k * P:(k + 1) * P],
                                          band_c[:, k, 0:BAND_HI[k] - BAND_LO[k]], start=(k == 0), stop=(k == KC - 1),
                                          skip_group_check=True)
                    e.wait_ge(s_ls, START + q * 4 - 1)
                    for k in range(KC):
                        mm = e.transpose(pb[1][:, k * P:(k + 1) * P], x1c[:, k, i * P:(i + 1) * P], ident[:])
                    mm.then_inc(s_lq, 1)

                def l1_slot(t, i, stages=3, last=False):
                    g = at_(e, gb + t)
                    q = e.snap(g * SUBS + i)
                    if i == 0:
                        e.wait_ge(s_lx, START + g + 1)
                    l1_stage1(q, i)
                    if stages > 1:
                        l1_stage2(e.snap(q - 1), (i - 1) % SUBS)
                    if stages > 2:
                        if i == 2:
                            e.wait_ge(s_lc, START + g + 1)
                        l1_stage3(e.snap(q - 2), (i - 2) % SUBS)

                walk_layer1(e, l1_slot)
                q = e.snap(end * SUBS)
                l1_stage2(e.snap(q - 1), SUBS - 1)
                l1_stage3(e.snap(q - 2), SUBS - 2)
                l1_stage3(e.snap(q - 1), SUBS - 1)

        @block.scalar
        def _(e):
            for counted in (s_lc, s_yn, s_ev, s_zev, s_aff, s_la, s_lb):
                e.sem_inc(counted, START)
            def act(out, in_, func, **kw):
                return e.activation(out, in_, func, **kw)

            def store_xbc(gx, c, halo):
                if halo:
                    e.wait_ge(s_tap, (gx - 1) * TPT + (c // 2 + 1) * TPP)
                    act(cb[:, c, 0:2, :], cb[:, c, ROWS:ROWS + 2, :], ACT.Copy).then_inc(s_ev, 1)
                    e.wait_ge(s_ev, START + (gx * XC + c) * 2 + 1)
                e.wait_ge(s_xbc, gx * XC + c + 1)
                act(cb[:, c, 2:ROWS + 2, 1:W + 1], pb[0][:].rearrange("p (r w) -> p r w", w=W), ACT.Copy
                    ).then_inc(s_ev, 1 if halo else 2)

            def silu(gx, u, c):
                e.wait_ge(s_tap, gx * TPT + (c // 2 + 1) * TPP)
                if c < ZC:
                    act(xs[:, u, c], xs[:, u, c], ACT.Silu, bias=b_conv[:, c:c + 1]).then_inc(s_silu, 1)
                else:
                    act(ct[:, u], xs[C_AT:C_AT + NS, u, c], ACT.Silu, bias=b_conv[C_AT:C_AT + NS, c:c + 1]).then_inc(s_silu, 1)
                    act(xs[0:NS, u, c], xs[0:NS, u, c], ACT.Silu, bias=b_conv[0:NS, c:c + 1]).then_inc(s_silu, 1)

            def silu_z(gx, h, q, free):
                e.wait_ge(s_op, START + free)
                e.wait_ge(s_z, gx * 6 + h * 3 + q + 1)
                act(gate[:, h, 2 * q:2 * q + 2].rearrange("p c n -> p (c n)"), pb[1][:], ACT.Silu).then_inc(s_zev, 1)

            def y_norm(sp):
                e.wait_ge(s_rs, START + sp * 2 + 2)
                act(y[:], y[:], ACT.Identity, bias=ln_rs[:, 1:2], scale=ln_rs[:, 0:1]).then_inc(s_yn, 1)

            def y_scale(sp):
                e.wait_ge(s_ynt, START + sp + 1)
                e.wait_ge(s_g, START + sp)
                for c in range(ZC):
                    a = act(aff[:, c], tr[:, c // KC, (c % KC) * P:(c % KC + 1) * P], ACT.Identity,
                            bias=chan[:, 1, c:c + 1], scale=chan[:, 0, c:c + 1])
                a.then_inc(s_aff, 1)

            e.wait_ge(s_const, 16 * len(CONSTS))
            act(neg_a[:], neg_a[:], ACT.Exp).then_inc(s_expa, 1)
            with e.Fori(0, NB) as b:
                gb = e.snap(b * TILES)
                e.wait_ge(s_r0p, b + 1)
                e.wait_ge(s_zero, b + 1)
                act(cb[:, :, 1, 1:W + 1], tr[:, 0, 0:XC * W].rearrange("p (c w) -> p c w", w=W), ACT.Copy).then_inc(s_r0, 1)
                for c in range(2):
                    store_xbc(gb, c, False)
                e.wait_ge(s_sp, b * SP_STEPS + 3)
                act(sp0[:], sp2[:], ACT.Exp).then_inc(s_dte, 1)
                for c in range(2, 4):
                    store_xbc(gb, c, False)
                for n, (dst, src) in enumerate(((e_from, yp[:, 0]), (e_to, yp[:, 1]), (e_all, ring[0][:]))):
                    e.wait_ge(s_sum, b * 3 + n + 1)
                    act(dst[:], src[:, 0:NSUB * HEADS], ACT.Exp).then_inc(s_exps, 1)
                for c in range(4, XC):
                    store_xbc(gb, c, False)
                e.wait_ge(s_yoff, START + gb * SUBS * 2)
                for c in range(XC):
                    silu(gb, 0, c)
                for c in range(2):
                    store_xbc(e.snap(gb + 1), c, True)
                for i in range(SUBS):
                    e.wait_ge(s_out[i], START + gb * 16)
                for q in range(3):
                    silu_z(gb, 0, q, gb * 4)

                def slot(t, u, i, first=False, left=TILES):
                    g = at_(e, gb + t)
                    s = e.snap(g * SUBS + i)
                    off, chunks = IN_PROJ[i]
                    chunks = chunks if off <= left else ()
                    if not first:
                        y_norm(e.snap(s - 1))
                    e.wait_ge(s_y, START + s)
                    for j in range(NG):
                        e.wait_ge(s_d, START + s * NG + j + 1)
                        act(mix[:, j], ring[j % 2][:], ACT.Exp).then_inc(s_e, 1)
                        if j == 0 and chunks:
                            store_xbc(e.snap(g + off), chunks[0], True)
                    if not first:
                        y_scale(e.snap(s - 1))
                    if len(chunks) > 1:
                        store_xbc(e.snap(g + off), chunks[1], True)
                    if i == 1:
                        silu_z(g, 1, 0, g * 4)
                    if i == 3 and left:
                        silu_z(e.snap(g + 1), 0, 0, g * 4 + 2)
                    if left:
                        if i == 3:
                            e.wait_ge(s_yoff, START + g * SUBS * 2)
                        for c in range(2 * i, min(2 * i + 2, XC)):
                            silu(e.snap(g + 1), 1 - u, c)
                    for q in range(1, 3):
                        if i == 1:
                            silu_z(g, 1, q, g * 4)
                        if i == 3 and left:
                            silu_z(e.snap(g + 1), 0, q, g * 4 + 2)

                walk_scan(e, gb, slot)
                end = e.snap(gb + TILES)
                y_norm(e.snap(end * SUBS - 1))
                y_scale(e.snap(end * SUBS - 1))

                e.wait_ge(s_gr, b * 2 + 2)

                def l1_squares(q, i):
                    e.wait_ge(s_lt, START + q + 1)
                    act(xg_t[:, i % 2], pb[0][:, 0:C], ACT.Copy).then_inc(s_la, 1)
                    act(sq_t[:, i % 2], pb[0][:, 0:C], ACT.Square).then_inc(s_la, 1)

                def l1_boxes(q, i):
                    e.wait_ge(s_lw, q + 1)
                    act(s2[:, i % 2], tr[:, 0, 0:C], ACT.Square).then_inc(s_lb, 1)
                    act(qw[:, i % 2], tr[:, 1, 0:C], ACT.Copy).then_inc(s_lb, 1)

                def l1_slot(t, i, stages=3, last=False):
                    g = at_(e, gb + t)
                    q = e.snap(g * SUBS + i)
                    l1_squares(q, i)
                    if stages > 1:
                        l1_boxes(e.snap(q - 1), (i - 1) % SUBS)
                    if i == 1:
                        e.wait_ge(s_lq, START + g * SUBS)
                        at = e.snap(t * TT) if not isinstance(t, int) else t * TT
                        act(x1c, xb[:, :, bass.ds(at, TT)], ACT.Copy).then_inc(s_lc, 1)

                walk_layer1(e, l1_slot)
                l1_boxes(e.snap(end * SUBS - 1), SUBS - 1)

        @block.vector
        def _(e):
            for counted in (s_lx, s_ls, s_sa, s_xtr, s_oev, s_g, s_lo, s_yr):
                e.sem_inc(counted, START)
            def gn_steps(n, entries):
                at = n * GN_STEPS
                e.memset(g_red[:], 0.0)
                for k in range(KC):
                    e.bn_aggr(mean_var[:, k], stats[:, k, 0:entries].rearrange("p n s -> p (n s)")).then_inc(s_gv, 1)
                e.wait_ge(s_gp, n * 4 + 1)
                e.tensor_scalar(g_red[:, 0:1], yp[0:GROUPS, 0, 0:1], 1.0 / GC, None, ALU.mult).then_inc(s_gv, 1)
                e.wait_ge(s_gp, n * 4 + 2)
                e.tensor_copy(g_mean[:], yp[:, 1, 0:KC]).then_inc(s_gv, 1)
                e.wait_ge(s_gv, at + 5)
                e.tensor_tensor(g_tmp[:], mean_var[:, :, 0], g_mean[:], ALU.subtract).then_inc(s_gv, 1)
                e.wait_ge(s_gv, at + 6)
                e.tensor_tensor(g_tmp[:], g_tmp[:], g_tmp[:], ALU.mult).then_inc(s_gv, 1)
                e.wait_ge(s_gv, at + 7)
                e.tensor_tensor(g_tmp[:], g_tmp[:], mean_var[:, :, 1], ALU.add).then_inc(s_gv, 1)
                e.wait_ge(s_gp, n * 4 + 3)
                e.tensor_scalar(g_red[:, 1:2], yp[0:GROUPS, 0, 1:2], 1.0 / GC, None, ALU.mult).then_inc(s_gv, 1)
                e.wait_ge(s_gp, n * 4 + 4)
                e.tensor_scalar(g_var[:], yp[:, 1, KC:2 * KC], EPS, None, ALU.add).then_inc(s_gv, 1)

            def conv(gx, u, pair, lo, hi):
                at = gx * TPT + pair * TPP
                for n in range(lo, hi):
                    tap, side = n // 2, n % 2
                    if 2 * pair + 1 < XC:
                        c, r0, r1 = 2 * pair + side, 0, ROWS
                    else:
                        c, r0, r1 = 2 * pair, side * ROWS // 2, (side + 1) * ROWS // 2
                    dy, dx = tap // 3, tap % 3
                    src = cb[:, c, r0 + dy:r1 + dy, dx:dx + W]
                    acc = xs[:, u, c, r0 * W:r1 * W].rearrange("p (r w) -> p r w", w=W)
                    if tap == 0:
                        if side == 0 or 2 * pair + 1 < XC:
                            e.wait_ge(s_ev, START + (gx * XC + c + 1) * 2)
                        ins = e.tensor_scalar(acc, src, w_conv[:, c, 0:1], None, ALU.mult)
                    else:
                        e.wait_ge(s_tap, at + n - 1)
                        ins = e.scalar_tensor_tensor(out=acc, in0=src, scalar=w_conv[:, c, tap:tap + 1], in1=acc,
                                                     op0=ALU.mult, op1=ALU.add)
                    ins.then_inc(s_tap, 1)

            def gate_rows(sp, gx, i):
                h = i // 2
                e.wait_ge(s_aff, START + sp + 1)
                e.wait_ge(s_zev, START + gx * 6 + h * 3 + 3)
                v = gate[:, h, :, (i % 2) * P:(i % 2 + 1) * P]
                e.tensor_tensor(v, v, aff[:], ALU.mult).then_inc(s_g, 1)

            def add_out(gx, tx, h, q):
                e.wait_ge(s_op, START + gx * 4 + h * 2 + q + 1)
                e.wait_ge(s_res[h], gx * 16 + 16)
                ms = ((0, 1), (2,))[q]
                at = tx * TT + h * HALF
                at = e.snap(at) if not isinstance(at, int) else at
                for n, m in enumerate(ms):
                    ins = e.tensor_tensor(xb[:, m, bass.ds(at, HALF)], pb[1][:, n * HALF:(n + 1) * HALF],
                                          xres[:, h, m], ALU.add)
                ins.then_inc(s_oev, 1)
                e.wait_ge(s_oev, START + gx * 4 + h * 2 + q + 1)
                entry = tx * 2 + h
                entry = e.snap(entry) if not isinstance(entry, int) else entry
                for m in ms:
                    e.bn_stats(stats[:, m, bass.ds(entry, 1)].rearrange("p a s -> p (a s)"), xb[:, m, bass.ds(at, HALF)]).then_inc(s_x1st, 1)

            e.memset(cb[:], 0.0)
            e.memset(xb[:, :, H * W:(H + 1) * W], 0.0).then_inc(s_setup, 1)
            e.wait_ge(s_const, 16 * len(CONSTS))
            for c in range(ZC):
                e.tensor_scalar(diag_d[:, c], ident[:], chan[:, 2, c:c + 1], None, ALU.mult).then_inc(s_setup, 1)
            e.wait_ge(s_expa, 1)
            e.tensor_scalar(neg_a[:], neg_a[:], -1.0, None, ALU.mult).then_inc(s_setup, 1)
            e.wait_ge(s_setup, ZC + 2)
            with e.Fori(0, NB) as b:
                gb = e.snap(b * TILES)
                e.wait_ge(s_yoff, START + gb * SUBS * 2)
                e.memset(cb[:, :, 0, :], 0.0)
                e.memset(state[:], 0.0).then_inc(s_zero, 1)
                e.wait_ge(s_x, (b + 1) * 16 * TILES)
                for t in range(TILES):
                    for k in range(KC):
                        e.bn_stats(stats[:, k, t], xb[:, k, t * TT:(t + 1) * TT]).then_inc(s_xst, 1)
                e.wait_ge(s_xst, (b + 1) * TILES * KC)
                n0 = e.snap(b * 2)
                gn_steps(n0, TILES)
                e.wait_ge(s_gr, n0 + 1)
                for lo, hi in ((0, 2 * TT), (2 * TT, H * W)):
                    for k in range(KC):
                        v = xb[:, k, lo:hi]
                        e.tensor_scalar(v, v, g_mean[:, k:k + 1], g_rstd[:, k:k + 1], ALU.subtract, ALU.mult
                                        ).then_inc(s_norm, 1)
                e.wait_ge(s_y, START + gb * SUBS)
                e.wait_ge(s_r0, b + 1)
                conv(gb, 0, 0, 0, TPP)
                at = e.snap(b * SP_STEPS)
                steps = [0]

                def step(ins):
                    steps[0] += 1
                    ins.then_inc(s_sp, 1)
                    e.wait_ge(s_sp, at + steps[0])

                def heads(v):
                    return v[:].unsqueeze(1).to_broadcast([P, NSUB, HEADS])

                def by_head(v):
                    return v[:].rearrange("p (n h) -> p n h", h=HEADS)

                e.wait_ge(s_dtp, b + 1)
                step(e.tensor_tensor(by_head(sp0), yp[:, 0, 0:NSUB * HEADS].rearrange("p (n h) -> p n h", h=HEADS),
                                     heads(dt_bias), ALU.add))
                step(e.tensor_scalar(sp1[:], sp0[:], 0.0, None, ALU.max))
                step(e.scalar_tensor_tensor(out=sp2[:], in0=sp1[:], scalar=-2.0, in1=sp0[:], op0=ALU.mult, op1=ALU.add))
                e.wait_ge(s_dte, b + 1)
                step(e.tensor_scalar(sp2[:], sp0[:], 2.0, None, ALU.add))
                step(e.reciprocal(sp2[:], sp2[:]))
                step(e.tensor_tensor(sp0[:], sp0[:], sp2[:], ALU.mult))
                step(e.tensor_tensor(sp2[:], sp0[:], sp0[:], ALU.mult))
                step(e.tensor_scalar(dt[:], sp2[:], 1.0 / (2 * LOG_TERMS + 1), None, ALU.mult))
                for n in range(LOG_TERMS - 1, 0, -1):
                    step(e.scalar_tensor_tensor(out=dt[:], in0=dt[:], scalar=1.0 / (2 * n + 1), in1=sp2[:],
                                                op0=ALU.add, op1=ALU.mult))
                step(e.scalar_tensor_tensor(out=dt[:], in0=dt[:], scalar=1.0, in1=sp0[:], op0=ALU.add, op1=ALU.mult))
                step(e.scalar_tensor_tensor(out=dt[:], in0=dt[:], scalar=2.0, in1=sp1[:], op0=ALU.mult, op1=ALU.add))
                step(e.tensor_tensor(by_head(a_dt), by_head(dt), heads(neg_a), ALU.mult))
                assert steps[0] == SP_STEPS, steps

                for pair in range(1, PAIRS):
                    conv(gb, 0, pair, 0, TPP)

                def slot(t, u, i, first=False, left=TILES):
                    g = at_(e, gb + t)
                    s = e.snap(g * SUBS + i)
                    at = e.snap((t * SUBS + i) * HEADS) if not isinstance(t, int) else (t * SUBS + i) * HEADS
                    e.wait_ge(s_xt, s + 1)
                    e.wait_ge(s_y, START + s)
                    e.wait_ge(s_xe, START + s)
                    dtv = dt[:, bass.ds(at, HEADS)]
                    for n in range(2):
                        e.tensor_tensor(x_dt[:, n * HB:(n + 1) * HB].rearrange("p (h d) -> p h d", d=HD),
                                        tr[:, n, 0:HB].rearrange("p (h d) -> p h d", d=HD),
                                        dtv[:, n * HEADS // 2:(n + 1) * HEADS // 2].unsqueeze(2).to_broadcast([P, HEADS // 2, HD]),
                                        ALU.mult)
                    e.tensor_copy(b_tok[:, i % 2], tr[:, 1, HB:HB + NS])
                    e.tensor_tensor(bc_m[:], tr[:, 0, HB:HB + P], upto[:], ALU.mult).then_inc(s_xtr, 1)
                    if left:
                        if i == 0:
                            e.wait_ge(s_y, START + g * SUBS)
                        g1 = e.snap(g + 1)
                        conv(g1, 1 - u, i, 0, 12)
                    for j in range(NG):
                        if j == 0:
                            e.wait_ge(s_xtr, START + s + 1)
                        e.wait_ge(s_e, s * NG + j + 1)
                        v = mix[:, j].rearrange("p (h l) -> p h l", h=HG)
                        e.tensor_tensor(v, v, bc_m[:].unsqueeze(1).to_broadcast([P, HG, P]), ALU.mult).then_inc(s_m, 1)
                    if not first:
                        gate_rows(e.snap(s - 1), g if i else e.snap(g - 1), (i - 1) % SUBS)
                    if left:
                        conv(g1, 1 - u, i, 12, TPP)
                    for n in range(2):
                        e.wait_ge(s_yoff, START + s * 2 + n + 1)
                        e.tensor_tensor(y_in[:, n * HB:(n + 1) * HB].rearrange("p (h d) -> p h d", d=HD),
                                        ring[1 - n][:, 0:HB].rearrange("p (h d) -> p h d", d=HD),
                                        e_from[:, bass.ds(at + n * HEADS // 2, HEADS // 2)].unsqueeze(2)
                                        .to_broadcast([P, HEADS // 2, HD]), ALU.mult).then_inc(s_t1, 1)
                    e.wait_ge(s_t1, s * 2 + 2)
                    e.wait_ge(s_ynt, START + s)
                    e.tensor_tensor(y[:].rearrange("p (n c) -> p n c", n=2), yp[:, :, 0:HB],
                                    y_in[:].rearrange("p (n c) -> p n c", n=2), ALU.add).then_inc(s_yr, 1)
                    e.wait_ge(s_yr, START + s + 1)
                    for n in range(2):
                        e.bn_stats(ln_st[:, n], y[:, n * HB:(n + 1) * HB]).then_inc(s_yst, 1)
                    for q in range(2):
                        if i == 0 and not first:
                            add_out(e.snap(g - 1), t - 1, 1, q)
                        if i == 2:
                            add_out(g, t, 0, q)
                    e.wait_ge(s_yst, s * 3 + 2)
                    e.wait_ge(s_ss, s + 1)
                    for n in range(2):
                        e.wait_ge(s_sn, START + s * 2 + n + 1)
                        v = state[:, n * HB:(n + 1) * HB]
                        e.tensor_tensor(v, ring[1 - n][0:NS, 0:HB], v, ALU.add).then_inc(s_sa, 1)
                        if n == 0:
                            e.bn_aggr(ln_mv[:], ln_st[:].rearrange("p n s -> p (n s)")).then_inc(s_yst, 1)
                    e.wait_ge(s_yst, s * 3 + 3)
                    e.wait_ge(s_rs, START + s * 2)
                    e.tensor_scalar(ln_vm[:, 1:2], ln_mv[:, 0:1], -1.0, None, ALU.mult)
                    e.tensor_scalar(ln_vm[:, 0:1], ln_mv[:, 1:2], EPS, None, ALU.add).then_inc(s_var, 1)

                walk_scan(e, gb, slot)
                end = e.snap(gb + TILES)
                last = e.snap(end - 1)
                gate_rows(e.snap(end * SUBS - 1), last, SUBS - 1)
                for q in range(2):
                    add_out(last, TILES - 1, 1, q)

                e.wait_ge(s_x1st, end * 2 * KC)
                n1 = e.snap(b * 2 + 1)
                gn_steps(n1, 2 * TILES)
                e.wait_ge(s_gr, n1 + 1)

                def l1_norm(g, t):
                    e.wait_ge(s_lt, START + g * SUBS)
                    at = e.snap(t * TT) if not isinstance(t, int) else t * TT
                    for k in range(KC):
                        ins = e.tensor_scalar(xg[:, k], xb[:, k, bass.ds(at, TT)], g_mean[:, k:k + 1], g_rstd[:, k:k + 1],
                                              ALU.subtract, ALU.mult)
                    ins.then_inc(s_lx, 1)

                def l1_ratio(q, g, i):
                    e.wait_ge(s_lq, START + q + 1)
                    e.tensor_scalar(den, l1_den(i)[:, 0:C], TINY, None, ALU.max).then_inc(s_ls, 1)
                    e.wait_ge(s_ls, START + q * 4 + 1)
                    e.reciprocal(rec, den).then_inc(s_ls, 1)
                    e.scalar_tensor_tensor(out=base, in0=den, scalar=TINY, in1=pb[1][:, 0:C], op0=ALU.is_le,
                                           op1=ALU.add).then_inc(s_ls, 1)
                    e.wait_ge(s_ls, START + q * 4 + 2)
                    e.tensor_tensor(ratio, l1_num(i)[:, 0:C], rec, ALU.mult).then_inc(s_ls, 1)
                    e.wait_ge(s_out[i], START + g * 16)
                    e.wait_ge(s_ls, START + q * 4 + 4)
                    e.tensor_tensor(out_b[:, i], ratio, base, ALU.add).then_inc(s_lo, 1)

                l1_norm(gb, 0)

                def l1_slot(t, i, stages=3, last=False):
                    g = at_(e, gb + t)
                    if stages > 2:
                        g2 = g if i >= 2 else e.snap(g - 1)
                        l1_ratio(e.snap(g * SUBS + i - 2), g2, (i - 2) % SUBS)
                    if i == SUBS - 1 and not last:
                        l1_norm(e.snap(g + 1), t + 1)

                walk_layer1(e, l1_slot)
                l1_ratio(e.snap(end * SUBS - 2), last, SUBS - 2)
                l1_ratio(e.snap(end * SUBS - 1), last, SUBS - 1)


def layout(x, w_in, w_conv, b_conv, dt_bias, a_log, d_param, gamma, beta, w_out):
    f = np.float32

    def by_partition(a, k):
        return np.ascontiguousarray(np.moveaxis(a.reshape(k, P, *a.shape[1:]), 0, 1))

    xbc = np.zeros((C, XC * P), f)
    xbc[:, 0:DI + NS] = w_in[:, DI:2 * DI + NS]
    xbc[:, DI + C_AT:DI + C_AT + NS] = w_in[:, 2 * DI + NS:2 * DI + 2 * NS]
    wc, bc = np.zeros((XC * P, TAPS), f), np.zeros((XC * P,), f)
    taps = w_conv.reshape(TAPS, -1).T
    wc[0:DI + NS], bc[0:DI + NS] = taps[0:DI + NS], b_conv[0:DI + NS]
    at = DI + C_AT
    wc[at:at + NS], bc[at:at + NS] = taps[DI + NS:], b_conv[DI + NS:]
    chan = np.stack([gamma.reshape(ZC, P), beta.reshape(ZC, P), np.repeat(d_param, HD).reshape(ZC, P)])
    k, m = np.arange(P)[:, None], np.arange(P)[None, :]
    ch, grp = np.arange(C), np.arange(GROUPS)
    to_group = (ch[:, None] // GC == grp[None, :]).astype(f)
    lo, hi = WIN_W // 2, WIN_W - WIN_W // 2 - 1
    band_w = ((k // W == m // W) & (k >= m - lo) & (k <= m + hi)).astype(f)
    count = band_w.sum(0, keepdims=True)
    lo, hi = WIN_C // 2, WIN_C - WIN_C // 2 - 1
    band = ((ch[:, None] >= ch[None, :] - lo) & (ch[:, None] <= ch[None, :] + hi)).astype(f)
    band_c = np.zeros((P, KC, BANDC), f)
    for n in range(KC):
        band_c[:, n, 0:BAND_HI[n] - BAND_LO[n]] = band[n * P:(n + 1) * P, BAND_LO[n]:BAND_HI[n]]
    xt = x.reshape(NB * TILES, TT, KC, P).transpose(0, 3, 2, 1)
    return {
        "x": np.ascontiguousarray(xt),
        "w_xbc": by_partition(xbc, KC), "w_z": by_partition(w_in[:, 0:DI], KC),
        "w_dt": by_partition(w_in[:, 2 * DI + 2 * NS:], KC), "w_out": by_partition(w_out, ZC),
        "w_conv": by_partition(wc, XC), "b_conv": by_partition(bc, XC),
        "chan": np.ascontiguousarray(chan.transpose(2, 0, 1)),
        "dt_bias": np.tile(dt_bias, (P, 1)), "neg_a": np.tile(a_log, (P, 1)),
        "upto": (k <= m).astype(f), "after": (k > m).astype(f), "ones": np.ones((P, P), f),
        "ident": np.eye(P, dtype=f), "to_group": by_partition(to_group, KC),
        "from_group": np.ascontiguousarray(to_group.T), "band_w": band_w, "band_wn": band_w * count, "band_c": band_c,
    }


def kernel(x, L0_conv_W_in, L0_conv_W_conv, L0_conv_b_conv, L0_conv_dt_bias, L0_conv_A_log, L0_conv_D_param,
           L0_conv_gamma, L0_conv_beta, L0_conv_W_out):
    import concourse.bacc as bacc
    from concourse.bass_utils import run_bass_kernel_spmd

    arrays = layout(*(np.asarray(v) for v in (
        x, L0_conv_W_in, L0_conv_W_conv, L0_conv_b_conv, L0_conv_dt_bias, L0_conv_A_log, L0_conv_D_param,
        L0_conv_gamma, L0_conv_beta, L0_conv_W_out)))
    nc = bacc.Bacc("TRN2", target_bir_lowering=False, num_devices=1)
    aps = {n: nc.dram_tensor(f"in_{n}", a.shape, mybir.dt.from_np(a.dtype), kind="ExternalInput").ap()
           for n, a in arrays.items()}
    aps["out"] = nc.dram_tensor("out", (NB * TILES, TT, C), F32, kind="ExternalOutput").ap()
    build(nc, aps)
    r = run_bass_kernel_spmd(nc, [{f"in_{n}": a for n, a in arrays.items()}], core_ids=[0])
    return r.results[0]["out"].reshape(NB, H, W, C)
```

```python
from contextlib import ExitStack

import numpy as np

import concourse.bass as bass
from concourse import mybir

F32 = mybir.dt.float32
F32R = mybir.dt.float32r
ALU = mybir.AluOpType
ACT = mybir.ActivationFunctionType

P = 128
NB, H, W, C = 8, 64, 64, 384
KC = C // P
HEADS, HD, NS = 12, 64, 16
DI = HEADS * HD
ZC = DI // P
XC = ZC + 1
C_AT = 32
ROWS = 8
TT = ROWS * W
TILES = H // ROWS
SUBS = TT // P
NSUB = TILES * SUBS
HG = 4
NG = HEADS // HG
HB = DI // 2
TAPS = 9
PAIRS = (XC + 1) // 2
TPP = 2 * TAPS
TPT = PAIRS * TPP
SPT = XC + 1
GROUPS = 32
GC = C // GROUPS
WIN_W, WIN_C = 5, 20
HALF = TT // 2
EPS = 1e-5
LOG_TERMS = 8
NORMS = 2 * KC
SP_STEPS = 12 + LOG_TERMS
GN_STEPS = 10
FIRST_POOL = (2, 3)
FIRST_STEPS = len(FIRST_POOL) * (2 * TAPS - 1)
START = 4
TINY = float(np.finfo(np.float32).tiny)
AHEAD = WIN_C - WIN_C // 2 - 1
BAND_LO = [0, P - AHEAD, 2 * P - AHEAD]
BAND_HI = [P + WIN_C // 2, 2 * P + WIN_C // 2, C]
BANDC = max(h - l for l, h in zip(BAND_LO, BAND_HI))
CONSTS = ["w_xbc", "w_z", "w_dt", "w_out", "w_conv", "b_conv", "chan", "dt_bias", "neg_a", "upto", "after", "ones",
          "ident", "to_group", "from_group", "band_w", "band_wn", "band_c"]
IN_PROJ = [(1, (2, 3)), (1, (4, 5)), (1, (6,)), (2, (0, 1))]


def at_(e, v):
    return v if isinstance(v, int) else e.snap(v)


def walk_scan(e, gb, slot):
    slot(0, 0, 0, first=True)
    with e.Fori(0, TILES // 2 - 1) as pair:
        t0 = e.snap(pair * 2)
        for k in range(1, 2 * SUBS + 1):
            slot(t0 + k // SUBS, (k // SUBS) % 2, k % SUBS)
    for k in range(1, 2 * SUBS):
        t = TILES - 2 + k // SUBS
        slot(t, t % 2, k % SUBS, left=TILES - 1 - t)


def walk_layer1(e, slot):
    for i in range(SUBS):
        slot(0, 0, i, stages=min(i + 1, 3))
    with e.Fori(0, TILES // 2 - 1) as pair:
        for u in (1, 0):
            t = e.snap(pair * 2 + 2 - u)
            for i in range(SUBS):
                slot(t, u, i)
    for i in range(SUBS):
        slot(TILES - 1, 1, i, last=True)


def build(nc, A):
    with ExitStack() as ctx:
        def sb(name, *shape, dtype=F32):
            return ctx.enter_context(nc.sbuf_tensor(name, list(shape), dtype))

        def sem(name):
            return ctx.enter_context(nc.semaphore(name))

        w_xbc = sb("w_xbc", P, KC, XC * P)
        w_z = sb("w_z", P, KC, DI)
        w_dt = sb("w_dt", P, KC, HEADS)
        w_out = sb("w_out", P, ZC, C)
        w_conv = sb("w_conv", P, XC, TAPS)
        b_conv = sb("b_conv", P, XC)
        chan = sb("chan", P, 3, ZC)
        dt_bias = sb("dt_bias", P, HEADS)
        neg_a = sb("neg_a", P, HEADS)
        upto = sb("upto", P, P)
        after = sb("after", P, P)
        ones = sb("ones", P, P)
        ident = sb("ident", P, P)
        to_group = sb("to_group", P, KC, GROUPS)
        from_group = sb("from_group", GROUPS, C)
        band_w = sb("band_w", P, P)
        band_wn = sb("band_wn", P, P)
        band_c = sb("band_c", P, KC, BANDC)
        diag_d = sb("diag_d", P, ZC, P)
        minus_half = sb("minus_half", P, KC)
        after_r = sb("after_r", P, P, dtype=F32R)

        xb = sb("xb", P, KC, (H + 1) * W)
        stats = sb("stats", P, KC, 2 * TILES, 6)
        mean_var = sb("mean_var", P, KC, 2)
        g_mean = sb("g_mean", P, KC)
        g_tmp = sb("g_tmp", P, KC)
        g_var = sb("g_var", P, KC)
        g_rstd = sb("g_rstd", P, KC)
        g_red = sb("g_red", GROUPS, 2)
        dt = sb("dt", P, NSUB * HEADS)
        a_dt = sb("a_dt", P, NSUB * HEADS)
        e_from = sb("e_from", P, NSUB * HEADS)
        e_to = sb("e_to", P, NSUB * HEADS)
        e_all = sb("e_all", P, NSUB * HEADS)
        a_hi = sb("a_hi", P, NSUB * HEADS, dtype=F32R)
        a_lo = sb("a_lo", P, NSUB * HEADS)

        cb = sb("cb", P, XC, ROWS + 2, W + 2)
        xs = sb("xs", P, 2, XC, TT)
        ct = sb("ct", NS, 2, TT)
        gate = sb("gate", P, 2, ZC, HALF)
        xres = sb("xres", P, 2, KC, HALF)

        a_tri = sb("a_tri", P, NG, 2, HG * P, dtype=F32R)
        mix = sb("mix", P, NG, HG * P)
        bc_m = sb("bc_m", P, P)
        b_tok = sb("b_tok", P, 2, NS)
        xd = sb("xd", P, 2, DI)
        x_dt, x_end = xd[:, 0], xd[:, 1]
        y_in = sb("y_in", P, DI)
        y = sb("y", P, DI)
        sp0, sp1, sp2 = a_lo, y[:, 0:NSUB * HEADS], y[:, NSUB * HEADS:2 * NSUB * HEADS]
        state = sb("state", NS, DI)
        ln_st = sb("ln_st", P, 2, 6)
        ln_mv = sb("ln_mv", P, 2)
        ln_vm = sb("ln_vm", P, 2)
        ln_rs = sb("ln_rs", P, 2)
        aff = sb("aff", P, ZC, P)

        gate_flat = gate[:].rearrange("p h c n -> p (h c n)")
        xg = [xd[:].rearrange("p u c -> p (u c)").rearrange("p (k n) -> p k n", k=KC),
              gate_flat[:, SUBS * C:].rearrange("p (k n) -> p k n", k=KC)]
        x1c = mix[:, :, :]
        out_b = gate_flat[:, 0:SUBS * C].rearrange("p (s c) -> p s c", s=SUBS)
        xs_flat = xs[:].rearrange("p u c n -> p (u c n)")

        def dt_rows(n):
            return xs[0:HEADS, 1, n % 4]

        def carve(n):
            return xs_flat[:, n * 2 * C:(n + 1) * 2 * C].rearrange("p (n c) -> p n c", n=2)

        xg_t, sq_t, s2, qw, den, ratio, x1_t = (carve(n) for n in range(7))
        rec, total, no_den = carve(7)[:, 0], carve(7)[:, 1], carve(8)[:, 0]

        pb = [ctx.enter_context(nc.psum_tensor(f"proj{i}", [P, 512], F32)) for i in range(2)]
        tr = ctx.enter_context(nc.psum_tensor("tr", [P, 2, 512], F32))
        ring = [ctx.enter_context(nc.psum_tensor(f"ring{i}", [P, 512], F32)) for i in range(2)]
        yp = ctx.enter_context(nc.psum_tensor("yp", [P, 2, 512], F32))


        def l1_num(i):
            return ring[0][:] if i % 2 == 0 else yp[:, 0]

        def l1_den(i):
            return ring[1][:] if i % 2 == 0 else yp[:, 1]

        s_const, s_setup = sem("consts_loaded"), sem("setup_done")
        s_half, s_expa = sem("minus_half_ready"), sem("exp_a_ready")
        s_x = sem("x_loaded")
        s_res = [sem(f"residual_loaded{h}") for h in range(2)]
        s_out = [sem(f"out_stored{i}") for i in range(SUBS)]
        s_xst = sem("x_stats")
        s_gp, s_gv, s_gr = sem("gn_summed"), sem("gn_step"), sem("gn_rstd")
        s_norm, s_zero = sem("x_normalised"), sem("image_zeroed")
        s_dtm, s_dtc = sem("dt_rows_projected"), sem("dt_rows_stored")
        s_dtp, s_sp, s_dte, s_sum, s_exps = (
            sem(n) for n in ("dt_transposed", "softplus_step", "dt_exp", "a_summed", "decays_ready"))
        s_r0p, s_r0 = sem("row0_projected"), sem("row0_stored")
        s_xbc, s_ev = sem("xbc_projected"), sem("xbc_stored")
        s_tap, s_silu = sem("conv_tap"), sem("silu_done")
        s_z, s_zev = sem("z_projected"), sem("z_stored")
        s_op, s_oev = sem("out_projected"), sem("out_added")
        s_x1st = sem("x1_stats")
        s_xt, s_xtr = sem("x_transposed"), sem("x_transposed_read")
        s_at, s_d, s_e, s_m = sem("a_tri_ready"), sem("decay_summed"), sem("decay_ready"), sem("mix_ready")
        s_y, s_yoff, s_t1 = sem("y_summed"), sem("y_of_state"), sem("y_of_state_read")
        s_xe, s_sn, s_ss, s_sa = sem("x_end_ready"), sem("state_product"), sem("state_scaled"), sem("state_added")
        s_yr, s_yst, s_var, s_rs, s_yn = sem("y_ready"), sem("y_stats"), sem("y_var"), sem("y_rstd"), sem("y_normed")
        s_ynt, s_aff, s_g = sem("y_transposed"), sem("y_scaled"), sem("gated")
        s_lx, s_lc = sem("l1_x_ready"), sem("l1_copy_ready")
        s_lt, s_la, s_lw, s_lb, s_lq = (
            sem(n) for n in ("l1_transposed", "l1_squares", "l1_box_w", "l1_box_read", "l1_box_c"))
        s_ls, s_lr, s_lbase, s_lo = sem("l1_step"), sem("l1_x1_read"), sem("l1_terms"), sem("l1_out")
        s_first = sem("conv_first_tile_step")

        block = ctx.enter_context(nc.Block())

        @block.sync
        def _(e):
            for counted in (*s_out,):
                e.sem_inc(counted, START)
            bufs = dict(w_xbc=w_xbc, w_z=w_z, w_dt=w_dt, w_out=w_out, w_conv=w_conv, b_conv=b_conv, chan=chan,
                        dt_bias=dt_bias, neg_a=neg_a, upto=upto, after=after, ones=ones, ident=ident,
                        to_group=to_group, from_group=from_group, band_w=band_w, band_wn=band_wn, band_c=band_c)
            for name in CONSTS:
                e.dma_start(bufs[name][:], A[name]).then_inc(s_const, 16)

            def load(g, t):
                at = t * TT if isinstance(t, int) else e.snap(t * TT)
                e.dma_start(xb[:, :, bass.ds(at, TT)], A["x"][bass.ds(g, 1)].rearrange("g p k n -> (g p) k n")
                            ).then_inc(s_x, 16)

            def image(gb, more):
                def slot(t, u, i, first=False, left=TILES):
                    g = at_(e, gb + t)
                    if i < 2:
                        e.wait_ge(s_xtr, START + g * SUBS + i + 1)
                        e.dma_start(xres[:, i], A["x"][bass.ds(g, 1), :, :, i * HALF:(i + 1) * HALF]
                                    .rearrange("g p k n -> (g p) k n")).then_inc(s_res[i], 16)

                walk_scan(e, gb, slot)
                with e.Fori(0, TILES) as t:
                    g = at_(e, gb + t)
                    if more:
                        e.wait_ge(s_lx, START + g + 1)
                        e.wait_ge(s_lc, START + g + 1)
                        load(e.snap(g + TILES), t)
                    for i in range(SUBS):
                        e.wait_ge(s_lo, START + g * SUBS + i + 1)
                        e.dma_start(A["out"][bass.ds(g, 1), i * P:(i + 1) * P].rearrange("g p c -> (g p) c"),
                                    out_b[:, i]).then_inc(s_out[i], 16)

            for t in range(TILES):
                load(t, t)
            if NB > 1:
                with e.Fori(0, NB - 1) as b:
                    image(e.snap(b * TILES), True)
            image((NB - 1) * TILES, False)
            for i in range(SUBS):
                e.wait_ge(s_out[i], START + 16 * NB * TILES)

        @block.gpsimd
        def _(e):
            for counted in (s_xe, s_rs, s_lo):
                e.sem_inc(counted, START)
            e.memset(minus_half[:], -0.5).then_inc(s_half, 1)
            e.wait_ge(s_half, 1)

            def root(n):
                e.wait_ge(s_gv, n * GN_STEPS + GN_STEPS)
                e.tensor_tensor(g_rstd[:], g_var[:], minus_half[:], ALU.pow).then_inc(s_gr, 1)

            def ln_root(sp):
                e.wait_ge(s_var, sp + 1)
                e.wait_ge(s_yn, START + sp)
                e.tensor_tensor(ln_rs[:, 0:1], ln_vm[:, 0:1], minus_half[:, 0:1], ALU.pow).then_inc(s_rs, 1)
                e.wait_ge(s_rs, START + sp * 2 + 1)
                e.tensor_tensor(ln_rs[:, 1:2], ln_vm[:, 1:2], ln_rs[:, 0:1], ALU.mult).then_inc(s_rs, 1)

            e.wait_ge(s_const, 16 * len(CONSTS))
            with e.Fori(0, NB) as b:
                gb = e.snap(b * TILES)
                root(e.snap(b * 2))
                e.wait_ge(s_lo, START + gb * SUBS)
                e.wait_ge(s_r0, b + 1)
                product = x_end[:, 0:TT].rearrange("p (r w) -> p r w", w=W)
                steps = [0]

                def first_step(ins):
                    steps[0] += 1
                    ins.then_inc(s_first, 1)
                    e.wait_ge(s_first, b * FIRST_STEPS + steps[0])

                for c in FIRST_POOL:
                    e.wait_ge(s_ev, START + (gb * XC + c + 1) * 2)
                    acc = xs[:, 0, c].rearrange("p (r w) -> p r w", w=W)
                    for tap in range(TAPS):
                        src = cb[:, c, tap // 3:ROWS + tap // 3, tap % 3:tap % 3 + W]
                        weight = w_conv[:, c, tap:tap + 1].unsqueeze(2).to_broadcast([P, ROWS, W])
                        first_step(e.tensor_tensor(product if tap else acc, src, weight, ALU.mult))
                        if tap:
                            first_step(e.tensor_tensor(acc, acc, product, ALU.add))
                assert steps[0] == FIRST_STEPS, steps
                e.wait_ge(s_sp, (b + 1) * SP_STEPS)
                e.wait_ge(s_exps, b * 3 + 3)

                def slot(t, u, i, first=False, left=TILES):
                    s = e.snap((gb + t) * SUBS + i)
                    at = e.snap((t * SUBS + i) * HEADS) if not isinstance(t, int) else (t * SUBS + i) * HEADS
                    e.wait_ge(s_d, START + s * NG)
                    for j in range(NG):
                        for part, src in enumerate((a_hi[:].bitcast(F32), a_lo[:])):
                            a = src[:, bass.ds(at + j * HG, HG)]
                            e.tensor_tensor(a_tri[:, j, part].rearrange("p (h l) -> p h l", h=HG),
                                            a.unsqueeze(2).to_broadcast([P, HG, P]),
                                            upto[:].unsqueeze(1).to_broadcast([P, HG, P]), ALU.mult).then_inc(s_at, 1)
                    if not first:
                        ln_root(e.snap(s - 1))
                    e.wait_ge(s_xtr, START + s + 1)
                    e.wait_ge(s_sn, START + s * 2)
                    e.tensor_tensor(x_end[:].rearrange("p (h d) -> p h d", h=HEADS),
                                    x_dt[:].rearrange("p (h d) -> p h d", h=HEADS),
                                    e_to[:, bass.ds(at, HEADS)].unsqueeze(2).to_broadcast([P, HEADS, HD]),
                                    ALU.mult).then_inc(s_xe, 1)
                    e.wait_ge(s_yoff, START + s * 2 + 2)
                    e.wait_ge(s_sa, START + s * 2)
                    sv = state[:].rearrange("p (h d) -> p h d", h=HEADS)
                    e.tensor_tensor(sv, sv, e_all[0:NS, bass.ds(at, HEADS)].unsqueeze(2).to_broadcast([NS, HEADS, HD]),
                                    ALU.mult).then_inc(s_ss, 1)

                walk_scan(e, gb, slot)
                ln_root(e.snap((gb + TILES) * SUBS - 1))
                root(e.snap(b * 2 + 1))

                def l1_add(q, g, i):
                    e.wait_ge(s_ls, START + q * 3 + 3)
                    e.wait_ge(s_lr, START + q + 1)
                    e.wait_ge(s_lo, START + q)
                    e.tensor_tensor(total, ratio[:, i % 2], x1_t[:, i % 2], ALU.add).then_inc(s_lbase, 1)
                    e.tensor_scalar(no_den, den[:, i % 2], TINY, None, ALU.is_le).then_inc(s_lbase, 1)
                    e.wait_ge(s_out[i], START + g * 16)
                    e.wait_ge(s_lbase, q * 2 + 2)
                    e.tensor_tensor(out_b[:, i], total, no_den, ALU.add).then_inc(s_lo, 1)

                def l1_slot(t, u, i, stages=3, last=False):
                    if stages > 2:
                        g = at_(e, gb + t)
                        l1_add(e.snap(g * SUBS + i - 2), g if i >= 2 else e.snap(g - 1), (i - 2) % SUBS)

                walk_layer1(e, l1_slot)
                end = e.snap(gb + TILES)
                for i in (SUBS - 2, SUBS - 1):
                    l1_add(e.snap((end - 1) * SUBS + i), e.snap(end - 1), i)

        @block.tensor
        def _(e):
            for counted in (s_d, s_sn, s_y, s_yoff, s_ynt, s_op, s_lq, s_lt):
                e.sem_inc(counted, START)
            def gn_sums(n):
                for r, ready in enumerate((3, 8)):
                    e.wait_ge(s_gv, n * GN_STEPS + ready)
                    for k in range(KC):
                        src = mean_var[:, k, 0:1] if r == 0 else g_tmp[:, k:k + 1]
                        mm = e.matmul(yp[0:GROUPS, 0, r:r + 1], to_group[:, k], src, start=(k == 0), stop=(k == KC - 1))
                    mm.then_inc(s_gp, 1)
                    e.wait_ge(s_gv, n * GN_STEPS + ready + 1)
                    for k in range(KC):
                        mm = e.matmul(yp[:, 1, KC * r + k:KC * r + k + 1], from_group[:, k * P:(k + 1) * P],
                                      g_red[:, r:r + 1], start=True, stop=True)
                    mm.then_inc(s_gp, 1)

            def in_proj(gx, tx, c):
                e.wait_ge(s_ev, START + (gx * XC + c) * 2)
                for k in range(KC):
                    mm = e.matmul(pb[0][:], w_xbc[:, k, c * P:(c + 1) * P], xb[:, k, bass.ds(tx * TT + W, TT)],
                                  start=(k == 0), stop=(k == KC - 1))
                mm.then_inc(s_xbc, 1)

            def z_proj(gx, tx, h, q, outs):
                e.wait_ge(s_zev, START + gx * 6 + h * 3 + q)
                e.wait_ge(s_oev, START + outs)
                for c in range(2):
                    for k in range(KC):
                        mm = e.matmul(pb[1][:, c * HALF:(c + 1) * HALF], w_z[:, k, (2 * q + c) * P:(2 * q + c + 1) * P],
                                      xb[:, k, bass.ds(tx * TT + h * HALF, HALF)], start=(k == 0), stop=(k == KC - 1))
                mm.then_inc(s_z, 1)

            def out_proj(gx, h, q, gated, zs):
                e.wait_ge(s_g, START + gated)
                e.wait_ge(s_zev, START + zs)
                e.wait_ge(s_oev, START + gx * 4 + h * 2 + q)
                for n, m in enumerate(((0, 1), (2,))[q]):
                    for k in range(ZC):
                        mm = e.matmul(pb[1][:, n * HALF:(n + 1) * HALF], w_out[:, k, m * P:(m + 1) * P], gate[:, h, k],
                                      start=(k == 0), stop=(k == ZC - 1))
                mm.then_inc(s_op, 1)

            def y_transpose(sp):
                e.wait_ge(s_yn, START + sp + 1)
                for c in range(ZC):
                    mm = e.transpose(tr[:, c // KC, (c % KC) * P:(c % KC + 1) * P], y[:, c * P:(c + 1) * P], ident[:])
                mm.then_inc(s_ynt, 1)

            e.wait_ge(s_const, 16 * len(CONSTS))
            with e.Fori(0, NB) as b:
                gb = e.snap(b * TILES)
                gn_sums(e.snap(b * 2))
                e.wait_ge(s_norm, b * NORMS + KC)
                e.wait_ge(s_zero, b + 1)
                for c in range(XC):
                    for k in range(KC):
                        mm = e.matmul(tr[:, 0, c * W:(c + 1) * W], w_xbc[:, k, c * P:(c + 1) * P], xb[:, k, 0:W],
                                      start=(k == 0), stop=(k == KC - 1))
                mm.then_inc(s_r0p, 1)
                for c in range(4):
                    in_proj(gb, 0, c)
                e.wait_ge(s_norm, (b + 1) * NORMS)
                def dt_transpose(n):
                    for i in range(SUBS):
                        at = (n * SUBS + i) * HEADS
                        mm = e.transpose(tr[:, 1, at:at + HEADS], dt_rows(n)[:, i * P:(i + 1) * P],
                                         ident[0:HEADS, 0:HEADS])
                    mm.then_inc(s_dtp, 1)

                for n in range(TILES):
                    for k in range(KC):
                        if k == 1 and n:
                            e.wait_ge(s_dtc, b * TILES + n)
                        mm = e.matmul(yp[0:HEADS, n % 2], w_dt[:, k], xb[:, k, n * TT:(n + 1) * TT],
                                      start=(k == 0), stop=(k == KC - 1))
                    mm.then_inc(s_dtm, 1)
                    if n:
                        dt_transpose(n - 1)
                e.wait_ge(s_dtc, (b + 1) * TILES)
                in_proj(gb, 0, 4)
                dt_transpose(TILES - 1)
                e.wait_ge(s_sp, (b + 1) * SP_STEPS - 2)
                for mask, bank in ((upto, yp[:, 0]), (after, yp[:, 1]), (ones, ring[0][:])):
                    e.matmul(bank[:, 0:NSUB * HEADS], mask[:], a_dt[:], start=True, stop=True).then_inc(s_sum, 1)
                for c in range(5, XC):
                    in_proj(gb, 0, c)
                for c in range(2):
                    in_proj(e.snap(gb + 1), 1, c)
                for q in range(3):
                    z_proj(gb, 0, 0, q, gb * 4)

                def slot(t, u, i, first=False, left=TILES):
                    g = at_(e, gb + t)
                    s = e.snap(g * SUBS + i)
                    tok = slice(i * P, (i + 1) * P)
                    off, chunks = IN_PROJ[i]
                    chunks = chunks if off <= left else ()
                    e.wait_ge(s_silu, (g + 1) * SPT)
                    e.wait_ge(s_xtr, START + s)
                    if first:
                        e.wait_ge(s_r0, b + 1)
                        e.wait_ge(s_exps, b * 3 + 3)
                    else:
                        e.wait_ge(s_aff, START + s - 1)
                    for c in range(ZC):
                        e.transpose(tr[:, c // KC, (c % KC) * P:(c % KC + 1) * P], xs[:, u, c, tok], ident[:])
                    e.transpose(tr[:, 1, HB:HB + NS], xs[0:NS, u, ZC, tok], ident[0:NS, 0:NS])
                    e.matmul(tr[:, 0, HB:HB + P], xs[0:NS, u, ZC, tok], ct[:, u, tok],
                             start=True, stop=True).then_inc(s_xt, 1)
                    if chunks:
                        in_proj(e.snap(g + off), e.snap(t + off), chunks[0])
                    if i == 1:
                        z_proj(g, t, 1, 0, g * 4)
                    if i == 3 and left:
                        z_proj(e.snap(g + 1), e.snap(t + 1), 0, 0, g * 4 + 2)
                    for j in range(NG):
                        if j == 0:
                            e.wait_ge(s_sa, START + s * 2)
                        if j == 2:
                            if not first:
                                e.wait_ge(s_xtr, START + s + 1)
                                y_transpose(e.snap(s - 1))
                            e.wait_ge(s_e, s * NG + 1)
                        e.wait_ge(s_at, (s * NG + j) * 2 + 2)
                        for part in range(2):
                            mm = e.matmul(ring[j % 2][:], after_r[:], a_tri[:, j, part], start=(part == 0),
                                          stop=(part == 1))
                        mm.then_inc(s_d, 1)
                    if len(chunks) > 1:
                        in_proj(e.snap(g + off), e.snap(t + off), chunks[1])
                    e.wait_ge(s_yr, START + s)
                    e.wait_ge(s_xtr, START + s + 1)
                    for c in range(ZC):
                        e.matmul(yp[:, c // KC, (c % KC) * P:(c % KC + 1) * P], xs[:, u, c, tok], diag_d[:, c],
                                 start=(c % KC == 0), stop=False, skip_group_check=True)
                    for h in range(HEADS):
                        if h % HG == 0:
                            e.wait_ge(s_m, s * NG + h // HG + 1)
                        at = (h % (HEADS // 2)) * HD
                        mm = e.matmul(yp[:, h // (HEADS // 2), at:at + HD],
                                      mix[:, h // HG, (h % HG) * P:(h % HG + 1) * P],
                                      x_dt[:, h * HD:(h + 1) * HD], start=False,
                                      stop=(h % (HEADS // 2) == HEADS // 2 - 1), skip_group_check=True)
                    mm.then_inc(s_y, 1)
                    if first:
                        e.wait_ge(s_zero, b + 1)
                    for n in range(2):
                        e.wait_ge(s_e, s * NG + n + 2)
                        e.matmul(ring[1 - n][:, 0:HB], ct[:, u, tok], state[:, n * HB:(n + 1) * HB],
                                 start=True, stop=True).then_inc(s_yoff, 1)
                    if i == 1:
                        z_proj(g, t, 1, 1, g * 4)
                    if i == 3 and left:
                        z_proj(e.snap(g + 1), e.snap(t + 1), 0, 1, g * 4 + 2)
                    e.wait_ge(s_xe, START + s + 1)
                    for n in range(2):
                        e.wait_ge(s_t1, s * 2 + n + 1)
                        e.matmul(ring[1 - n][0:NS, 0:HB], b_tok[:, i % 2], x_end[:, n * HB:(n + 1) * HB],
                                 start=True, stop=True).then_inc(s_sn, 1)
                    if i == 1:
                        z_proj(g, t, 1, 2, g * 4)
                    if i == 3 and left:
                        z_proj(e.snap(g + 1), e.snap(t + 1), 0, 2, g * 4 + 2)
                    for q in range(2):
                        if i == 0 and not first:
                            out_proj(e.snap(g - 1), 1, q, s, g * 6 + 3)
                        if i == 2:
                            out_proj(g, 0, q, s, g * 6 + 6)

                walk_scan(e, gb, slot)
                end = e.snap(gb + TILES)
                y_transpose(e.snap(end * SUBS - 1))
                for q in range(2):
                    out_proj(e.snap(end - 1), 1, q, end * SUBS, end * 6)

                gn_sums(e.snap(b * 2 + 1))

                def l1_stage1(q, u, i):
                    e.wait_ge(s_la, START + q * 2)
                    for k in range(KC):
                        mm = e.transpose(pb[0][:, k * P:(k + 1) * P], xg[u][:, k, i * P:(i + 1) * P], ident[:])
                    mm.then_inc(s_lt, 1)

                def l1_stage2(q, i):
                    e.wait_ge(s_la, START + q * 2 + 2)
                    e.wait_ge(s_lb, START + q * 2)
                    for src, band, n in ((xg_t, band_w, 0), (sq_t, band_wn, 1)):
                        for k in range(KC):
                            mm = e.matmul(tr[:, n, k * P:(k + 1) * P], src[:, i % 2, k * P:(k + 1) * P], band[:],
                                          start=True, stop=True)
                    mm.then_inc(s_lw, 1)

                def l1_stage3(q, i):
                    e.wait_ge(s_lb, START + q * 2 + 2)
                    e.wait_ge(s_ls, START + q * 3 - 3)
                    for src, bank in ((qw, l1_den(i)), (s2, l1_num(i))):
                        for k in range(KC):
                            mm = e.matmul(bank[:, BAND_LO[k]:BAND_HI[k]], src[:, i % 2, k * P:(k + 1) * P],
                                          band_c[:, k, 0:BAND_HI[k] - BAND_LO[k]], start=(k == 0), stop=(k == KC - 1),
                                          skip_group_check=True)
                    e.wait_ge(s_lr, START + q)
                    for k in range(KC):
                        mm = e.transpose(pb[1][:, k * P:(k + 1) * P], x1c[:, k, i * P:(i + 1) * P], ident[:])
                    mm.then_inc(s_lq, 1)

                def l1_slot(t, u, i, stages=3, last=False):
                    g = at_(e, gb + t)
                    q = e.snap(g * SUBS + i)
                    if i == 0:
                        e.wait_ge(s_lx, START + g + 1)
                    l1_stage1(q, u, i)
                    if stages > 1:
                        l1_stage2(e.snap(q - 1), (i - 1) % SUBS)
                    if stages > 2:
                        if i == 2:
                            e.wait_ge(s_lc, START + g + 1)
                        l1_stage3(e.snap(q - 2), (i - 2) % SUBS)

                walk_layer1(e, l1_slot)
                q = e.snap(end * SUBS)
                l1_stage2(e.snap(q - 1), SUBS - 1)
                l1_stage3(e.snap(q - 2), SUBS - 2)
                l1_stage3(e.snap(q - 1), SUBS - 1)

        @block.scalar
        def _(e):
            for counted in (s_lc, s_yn, s_ev, s_zev, s_aff, s_la, s_lb, s_lr):
                e.sem_inc(counted, START)
            def act(out, in_, func, **kw):
                return e.activation(out, in_, func, **kw)

            def store_xbc(gx, c, halo):
                if halo:
                    e.wait_ge(s_tap, (gx - 1) * TPT + (c // 2 + 1) * TPP)
                    act(cb[:, c, 0:2, :], cb[:, c, ROWS:ROWS + 2, :], ACT.Copy).then_inc(s_ev, 1)
                    e.wait_ge(s_ev, START + (gx * XC + c) * 2 + 1)
                e.wait_ge(s_xbc, gx * XC + c + 1)
                act(cb[:, c, 2:ROWS + 2, 1:W + 1], pb[0][:].rearrange("p (r w) -> p r w", w=W), ACT.Copy
                    ).then_inc(s_ev, 1 if halo else 2)

            def silu(gx, u, c):
                e.wait_ge(s_tap, gx * TPT + (c // 2 + 1) * TPP)
                if c < ZC:
                    act(xs[:, u, c], xs[:, u, c], ACT.Silu, bias=b_conv[:, c:c + 1]).then_inc(s_silu, 1)
                else:
                    act(ct[:, u], xs[C_AT:C_AT + NS, u, c], ACT.Silu, bias=b_conv[C_AT:C_AT + NS, c:c + 1]).then_inc(s_silu, 1)
                    act(xs[0:NS, u, c], xs[0:NS, u, c], ACT.Silu, bias=b_conv[0:NS, c:c + 1]).then_inc(s_silu, 1)

            def silu_z(gx, h, q, free):
                e.wait_ge(s_op, START + free)
                e.wait_ge(s_z, gx * 6 + h * 3 + q + 1)
                act(gate[:, h, 2 * q:2 * q + 2].rearrange("p c n -> p (c n)"), pb[1][:], ACT.Silu).then_inc(s_zev, 1)

            def y_norm(sp):
                e.wait_ge(s_rs, START + sp * 2 + 2)
                act(y[:], y[:], ACT.Identity, bias=ln_rs[:, 1:2], scale=ln_rs[:, 0:1]).then_inc(s_yn, 1)

            def y_scale(sp):
                e.wait_ge(s_ynt, START + sp + 1)
                e.wait_ge(s_g, START + sp)
                for c in range(ZC):
                    a = act(aff[:, c], tr[:, c // KC, (c % KC) * P:(c % KC + 1) * P], ACT.Identity,
                            bias=chan[:, 1, c:c + 1], scale=chan[:, 0, c:c + 1])
                a.then_inc(s_aff, 1)

            e.wait_ge(s_const, 16 * len(CONSTS))
            act(neg_a[:], neg_a[:], ACT.Exp).then_inc(s_expa, 1)
            with e.Fori(0, NB) as b:
                gb = e.snap(b * TILES)
                e.wait_ge(s_r0p, b + 1)
                e.wait_ge(s_zero, b + 1)
                act(cb[:, :, 1, 1:W + 1], tr[:, 0, 0:XC * W].rearrange("p (c w) -> p c w", w=W), ACT.Copy).then_inc(s_r0, 1)
                for c in range(4):
                    store_xbc(gb, c, False)
                e.wait_ge(s_lo, START + gb * SUBS)
                for n in range(TILES):
                    e.wait_ge(s_dtm, b * TILES + n + 1)
                    if n >= 4:
                        e.wait_ge(s_dtp, b * TILES + n - 3)
                    act(dt_rows(n), yp[0:HEADS, n % 2], ACT.Copy).then_inc(s_dtc, 1)
                store_xbc(gb, 4, False)
                e.wait_ge(s_sp, b * SP_STEPS + 3)
                act(sp0[:], sp2, ACT.Exp).then_inc(s_dte, 1)
                for n, (dst, src) in enumerate(((e_from, yp[:, 0]), (e_to, yp[:, 1]), (e_all, ring[0][:]))):
                    e.wait_ge(s_sum, b * 3 + n + 1)
                    act(dst[:], src[:, 0:NSUB * HEADS], ACT.Exp).then_inc(s_exps, 1)
                for c in range(5, XC):
                    store_xbc(gb, c, False)
                e.wait_ge(s_yoff, START + gb * SUBS * 2)
                for c in range(2):
                    silu(gb, 0, c)
                    store_xbc(e.snap(gb + 1), c, True)
                for i in range(SUBS):
                    e.wait_ge(s_out[i], START + gb * 16)
                for q in range(3):
                    silu_z(gb, 0, q, gb * 4)
                e.wait_ge(s_first, (b + 1) * FIRST_STEPS)
                for c in range(2, XC):
                    silu(gb, 0, c)

                def slot(t, u, i, first=False, left=TILES):
                    g = at_(e, gb + t)
                    s = e.snap(g * SUBS + i)
                    off, chunks = IN_PROJ[i]
                    chunks = chunks if off <= left else ()
                    if not first:
                        y_norm(e.snap(s - 1))
                    e.wait_ge(s_y, START + s)
                    for j in range(NG):
                        e.wait_ge(s_d, START + s * NG + j + 1)
                        act(mix[:, j], ring[j % 2][:], ACT.Exp).then_inc(s_e, 1)
                        if j == 0 and chunks:
                            store_xbc(e.snap(g + off), chunks[0], True)
                    if not first:
                        y_scale(e.snap(s - 1))
                    if len(chunks) > 1:
                        store_xbc(e.snap(g + off), chunks[1], True)
                    if i == 1:
                        silu_z(g, 1, 0, g * 4)
                    if i == 3 and left:
                        silu_z(e.snap(g + 1), 0, 0, g * 4 + 2)
                    if left:
                        if i == 3:
                            e.wait_ge(s_yoff, START + g * SUBS * 2)
                        for c in range(2 * i, min(2 * i + 2, XC)):
                            silu(e.snap(g + 1), 1 - u, c)
                    for q in range(1, 3):
                        if i == 1:
                            silu_z(g, 1, q, g * 4)
                        if i == 3 and left:
                            silu_z(e.snap(g + 1), 0, q, g * 4 + 2)

                walk_scan(e, gb, slot)
                end = e.snap(gb + TILES)
                y_norm(e.snap(end * SUBS - 1))
                y_scale(e.snap(end * SUBS - 1))

                e.wait_ge(s_gr, b * 2 + 2)

                def l1_squares(q, i):
                    e.wait_ge(s_lt, START + q + 1)
                    act(xg_t[:, i % 2], pb[0][:, 0:C], ACT.Copy).then_inc(s_la, 1)
                    act(sq_t[:, i % 2], pb[0][:, 0:C], ACT.Square).then_inc(s_la, 1)

                def l1_boxes(q, i):
                    e.wait_ge(s_lw, q + 1)
                    act(s2[:, i % 2], tr[:, 0, 0:C], ACT.Square).then_inc(s_lb, 1)
                    act(qw[:, i % 2], tr[:, 1, 0:C], ACT.Copy).then_inc(s_lb, 1)

                def l1_x1(q, i):
                    e.wait_ge(s_lq, START + q + 1)
                    e.wait_ge(s_lo, START + q - 1)
                    act(x1_t[:, i % 2], pb[1][:, 0:C], ACT.Copy).then_inc(s_lr, 1)

                def l1_slot(t, u, i, stages=3, last=False):
                    g = at_(e, gb + t)
                    q = e.snap(g * SUBS + i)
                    l1_squares(q, i)
                    if stages > 1:
                        l1_boxes(e.snap(q - 1), (i - 1) % SUBS)
                    if stages > 2:
                        l1_x1(e.snap(q - 2), (i - 2) % SUBS)
                    if i == 1:
                        e.wait_ge(s_lq, START + g * SUBS)
                        at = e.snap(t * TT) if not isinstance(t, int) else t * TT
                        act(x1c, xb[:, :, bass.ds(at, TT)], ACT.Copy).then_inc(s_lc, 1)

                walk_layer1(e, l1_slot)
                l1_boxes(e.snap(end * SUBS - 1), SUBS - 1)
                for i in (SUBS - 2, SUBS - 1):
                    l1_x1(e.snap((end - 1) * SUBS + i), i)

        @block.vector
        def _(e):
            for counted in (s_lx, s_ls, s_sa, s_xtr, s_oev, s_g, s_yr):
                e.sem_inc(counted, START)
            def gn_steps(n, entries):
                at = n * GN_STEPS
                e.memset(g_red[:], 0.0)
                for k in range(KC):
                    e.bn_aggr(mean_var[:, k], stats[:, k, 0:entries].rearrange("p n s -> p (n s)")).then_inc(s_gv, 1)
                e.wait_ge(s_gp, n * 4 + 1)
                e.tensor_scalar(g_red[:, 0:1], yp[0:GROUPS, 0, 0:1], 1.0 / GC, None, ALU.mult).then_inc(s_gv, 1)
                e.wait_ge(s_gp, n * 4 + 2)
                e.tensor_copy(g_mean[:], yp[:, 1, 0:KC]).then_inc(s_gv, 1)
                e.wait_ge(s_gv, at + 5)
                e.tensor_tensor(g_tmp[:], mean_var[:, :, 0], g_mean[:], ALU.subtract).then_inc(s_gv, 1)
                e.wait_ge(s_gv, at + 6)
                e.tensor_tensor(g_tmp[:], g_tmp[:], g_tmp[:], ALU.mult).then_inc(s_gv, 1)
                e.wait_ge(s_gv, at + 7)
                e.tensor_tensor(g_tmp[:], g_tmp[:], mean_var[:, :, 1], ALU.add).then_inc(s_gv, 1)
                e.wait_ge(s_gp, n * 4 + 3)
                e.tensor_scalar(g_red[:, 1:2], yp[0:GROUPS, 0, 1:2], 1.0 / GC, None, ALU.mult).then_inc(s_gv, 1)
                e.wait_ge(s_gp, n * 4 + 4)
                e.tensor_scalar(g_var[:], yp[:, 1, KC:2 * KC], EPS, None, ALU.add).then_inc(s_gv, 1)

            def conv(gx, u, pair, lo, hi):
                at = gx * TPT + pair * TPP
                for n in range(lo, hi):
                    tap, side = n // 2, n % 2
                    if 2 * pair + 1 < XC:
                        c, r0, r1 = 2 * pair + side, 0, ROWS
                    else:
                        c, r0, r1 = 2 * pair, side * ROWS // 2, (side + 1) * ROWS // 2
                    dy, dx = tap // 3, tap % 3
                    src = cb[:, c, r0 + dy:r1 + dy, dx:dx + W]
                    acc = xs[:, u, c, r0 * W:r1 * W].rearrange("p (r w) -> p r w", w=W)
                    if tap == 0:
                        if side == 0 or 2 * pair + 1 < XC:
                            e.wait_ge(s_ev, START + (gx * XC + c + 1) * 2)
                        ins = e.tensor_scalar(acc, src, w_conv[:, c, 0:1], None, ALU.mult)
                    else:
                        e.wait_ge(s_tap, at + n - 1)
                        ins = e.scalar_tensor_tensor(out=acc, in0=src, scalar=w_conv[:, c, tap:tap + 1], in1=acc,
                                                     op0=ALU.mult, op1=ALU.add)
                    ins.then_inc(s_tap, 1)

            def gate_rows(sp, gx, i):
                h = i // 2
                e.wait_ge(s_aff, START + sp + 1)
                e.wait_ge(s_zev, START + gx * 6 + h * 3 + 3)
                v = gate[:, h, :, (i % 2) * P:(i % 2 + 1) * P]
                e.tensor_tensor(v, v, aff[:], ALU.mult).then_inc(s_g, 1)

            def add_out(gx, tx, h, q):
                e.wait_ge(s_op, START + gx * 4 + h * 2 + q + 1)
                e.wait_ge(s_res[h], gx * 16 + 16)
                ms = ((0, 1), (2,))[q]
                at = tx * TT + h * HALF
                at = e.snap(at) if not isinstance(at, int) else at
                for n, m in enumerate(ms):
                    ins = e.tensor_tensor(xb[:, m, bass.ds(at, HALF)], pb[1][:, n * HALF:(n + 1) * HALF],
                                          xres[:, h, m], ALU.add)
                ins.then_inc(s_oev, 1)
                e.wait_ge(s_oev, START + gx * 4 + h * 2 + q + 1)
                entry = tx * 2 + h
                entry = e.snap(entry) if not isinstance(entry, int) else entry
                for m in ms:
                    e.bn_stats(stats[:, m, bass.ds(entry, 1)].rearrange("p a s -> p (a s)"), xb[:, m, bass.ds(at, HALF)]).then_inc(s_x1st, 1)

            e.memset(cb[:], 0.0)
            e.memset(xb[:, :, H * W:(H + 1) * W], 0.0).then_inc(s_setup, 1)
            e.wait_ge(s_const, 16 * len(CONSTS))
            for c in range(ZC):
                e.tensor_scalar(diag_d[:, c], ident[:], chan[:, 2, c:c + 1], None, ALU.mult).then_inc(s_setup, 1)
            e.wait_ge(s_expa, 1)
            e.tensor_copy(after_r[:], after[:]).then_inc(s_setup, 1)
            e.tensor_scalar(neg_a[:], neg_a[:], -1.0, None, ALU.mult).then_inc(s_setup, 1)
            e.wait_ge(s_setup, ZC + 3)
            with e.Fori(0, NB) as b:
                gb = e.snap(b * TILES)
                e.wait_ge(s_yoff, START + gb * SUBS * 2)
                e.memset(cb[:, :, 0, :], 0.0)
                e.memset(state[:], 0.0).then_inc(s_zero, 1)
                e.wait_ge(s_x, (b + 1) * 16 * TILES)
                for t in range(TILES):
                    for k in range(KC):
                        e.bn_stats(stats[:, k, t], xb[:, k, t * TT:(t + 1) * TT]).then_inc(s_xst, 1)
                e.wait_ge(s_xst, (b + 1) * TILES * KC)
                n0 = e.snap(b * 2)
                gn_steps(n0, TILES)
                e.wait_ge(s_gr, n0 + 1)
                for lo, hi in ((0, 2 * TT), (2 * TT, H * W)):
                    for k in range(KC):
                        v = xb[:, k, lo:hi]
                        e.tensor_scalar(v, v, g_mean[:, k:k + 1], g_rstd[:, k:k + 1], ALU.subtract, ALU.mult
                                        ).then_inc(s_norm, 1)
                e.wait_ge(s_lo, START + gb * SUBS)
                e.wait_ge(s_r0, b + 1)
                conv(gb, 0, 0, 0, TPP)
                at = e.snap(b * SP_STEPS)
                steps = [0]

                def step(ins):
                    steps[0] += 1
                    ins.then_inc(s_sp, 1)
                    e.wait_ge(s_sp, at + steps[0])

                def heads(v):
                    return v[:].unsqueeze(1).to_broadcast([P, NSUB, HEADS])

                def by_head(v):
                    return v[:].rearrange("p (n h) -> p n h", h=HEADS)

                e.wait_ge(s_dtp, (b + 1) * TILES)
                step(e.tensor_tensor(by_head(sp0), tr[:, 1, 0:NSUB * HEADS].rearrange("p (n h) -> p n h", h=HEADS),
                                     heads(dt_bias), ALU.add))
                step(e.tensor_scalar(sp1, sp0[:], 0.0, None, ALU.max))
                step(e.scalar_tensor_tensor(out=sp2, in0=sp1, scalar=-2.0, in1=sp0[:], op0=ALU.mult, op1=ALU.add))
                e.wait_ge(s_dte, b + 1)
                step(e.tensor_scalar(sp2, sp0[:], 2.0, None, ALU.add))
                step(e.reciprocal(sp2, sp2))
                step(e.tensor_tensor(sp0[:], sp0[:], sp2, ALU.mult))
                step(e.tensor_tensor(sp2, sp0[:], sp0[:], ALU.mult))
                step(e.tensor_scalar(dt[:], sp2, 1.0 / (2 * LOG_TERMS + 1), None, ALU.mult))
                for n in range(LOG_TERMS - 1, 0, -1):
                    step(e.scalar_tensor_tensor(out=dt[:], in0=dt[:], scalar=1.0 / (2 * n + 1), in1=sp2,
                                                op0=ALU.add, op1=ALU.mult))
                step(e.scalar_tensor_tensor(out=dt[:], in0=dt[:], scalar=1.0, in1=sp0[:], op0=ALU.add, op1=ALU.mult))
                step(e.scalar_tensor_tensor(out=dt[:], in0=dt[:], scalar=2.0, in1=sp1, op0=ALU.mult, op1=ALU.add))
                step(e.tensor_tensor(by_head(a_dt), by_head(dt), heads(neg_a), ALU.mult))
                step(e.tensor_copy(a_hi[:], a_dt[:]))
                step(e.tensor_tensor(a_lo[:], a_dt[:], a_hi[:].bitcast(F32), ALU.subtract))
                assert steps[0] == SP_STEPS, steps

                for pair in range(1, PAIRS):
                    if 2 * pair in FIRST_POOL:
                        e.wait_ge(s_tap, gb * TPT + pair * TPP)
                        e.sem_inc(s_tap, TPP)
                    else:
                        conv(gb, 0, pair, 0, TPP)

                def slot(t, u, i, first=False, left=TILES):
                    g = at_(e, gb + t)
                    s = e.snap(g * SUBS + i)
                    at = e.snap((t * SUBS + i) * HEADS) if not isinstance(t, int) else (t * SUBS + i) * HEADS
                    e.wait_ge(s_xt, s + 1)
                    e.wait_ge(s_y, START + s)
                    e.wait_ge(s_xe, START + s)
                    dtv = dt[:, bass.ds(at, HEADS)]
                    for n in range(2):
                        e.tensor_tensor(x_dt[:, n * HB:(n + 1) * HB].rearrange("p (h d) -> p h d", d=HD),
                                        tr[:, n, 0:HB].rearrange("p (h d) -> p h d", d=HD),
                                        dtv[:, n * HEADS // 2:(n + 1) * HEADS // 2].unsqueeze(2).to_broadcast([P, HEADS // 2, HD]),
                                        ALU.mult)
                    e.tensor_copy(b_tok[:, i % 2], tr[:, 1, HB:HB + NS])
                    e.tensor_tensor(bc_m[:], tr[:, 0, HB:HB + P], upto[:], ALU.mult).then_inc(s_xtr, 1)
                    if left:
                        if i == 0:
                            e.wait_ge(s_y, START + g * SUBS)
                        g1 = e.snap(g + 1)
                        conv(g1, 1 - u, i, 0, 12)
                    for j in range(NG):
                        if j == 0:
                            e.wait_ge(s_xtr, START + s + 1)
                        e.wait_ge(s_e, s * NG + j + 1)
                        v = mix[:, j].rearrange("p (h l) -> p h l", h=HG)
                        e.tensor_tensor(v, v, bc_m[:].unsqueeze(1).to_broadcast([P, HG, P]), ALU.mult).then_inc(s_m, 1)
                    if not first:
                        gate_rows(e.snap(s - 1), g if i else e.snap(g - 1), (i - 1) % SUBS)
                    if left:
                        conv(g1, 1 - u, i, 12, TPP)
                    for n in range(2):
                        e.wait_ge(s_yoff, START + s * 2 + n + 1)
                        e.tensor_tensor(y_in[:, n * HB:(n + 1) * HB].rearrange("p (h d) -> p h d", d=HD),
                                        ring[1 - n][:, 0:HB].rearrange("p (h d) -> p h d", d=HD),
                                        e_from[:, bass.ds(at + n * HEADS // 2, HEADS // 2)].unsqueeze(2)
                                        .to_broadcast([P, HEADS // 2, HD]), ALU.mult).then_inc(s_t1, 1)
                    e.wait_ge(s_t1, s * 2 + 2)
                    e.wait_ge(s_ynt, START + s)
                    e.tensor_tensor(y[:].rearrange("p (n c) -> p n c", n=2), yp[:, :, 0:HB],
                                    y_in[:].rearrange("p (n c) -> p n c", n=2), ALU.add).then_inc(s_yr, 1)
                    e.wait_ge(s_yr, START + s + 1)
                    for n in range(2):
                        e.bn_stats(ln_st[:, n], y[:, n * HB:(n + 1) * HB]).then_inc(s_yst, 1)
                    for q in range(2):
                        if i == 0 and not first:
                            add_out(e.snap(g - 1), t - 1, 1, q)
                        if i == 2:
                            add_out(g, t, 0, q)
                    e.wait_ge(s_yst, s * 3 + 2)
                    e.wait_ge(s_ss, s + 1)
                    for n in range(2):
                        e.wait_ge(s_sn, START + s * 2 + n + 1)
                        v = state[:, n * HB:(n + 1) * HB]
                        e.tensor_tensor(v, ring[1 - n][0:NS, 0:HB], v, ALU.add).then_inc(s_sa, 1)
                        if n == 0:
                            e.bn_aggr(ln_mv[:], ln_st[:].rearrange("p n s -> p (n s)")).then_inc(s_yst, 1)
                    e.wait_ge(s_yst, s * 3 + 3)
                    e.wait_ge(s_rs, START + s * 2)
                    e.tensor_scalar(ln_vm[:, 1:2], ln_mv[:, 0:1], -1.0, None, ALU.mult)
                    e.tensor_scalar(ln_vm[:, 0:1], ln_mv[:, 1:2], EPS, None, ALU.add).then_inc(s_var, 1)

                walk_scan(e, gb, slot)
                end = e.snap(gb + TILES)
                last = e.snap(end - 1)
                gate_rows(e.snap(end * SUBS - 1), last, SUBS - 1)
                for q in range(2):
                    add_out(last, TILES - 1, 1, q)

                e.wait_ge(s_x1st, end * 2 * KC)
                n1 = e.snap(b * 2 + 1)
                gn_steps(n1, 2 * TILES)
                e.wait_ge(s_gr, n1 + 1)

                def l1_norm(t, u):
                    at = e.snap(t * TT) if not isinstance(t, int) else t * TT
                    for k in range(KC):
                        ins = e.tensor_scalar(xg[u][:, k], xb[:, k, bass.ds(at, TT)], g_mean[:, k:k + 1], g_rstd[:, k:k + 1],
                                              ALU.subtract, ALU.mult)
                    ins.then_inc(s_lx, 1)

                def l1_ratio(q, g, i):
                    e.wait_ge(s_lq, START + q + 1)
                    e.wait_ge(s_lo, START + q - 1)
                    e.tensor_scalar(den[:, i % 2], l1_den(i)[:, 0:C], TINY, None, ALU.max).then_inc(s_ls, 1)
                    e.wait_ge(s_ls, START + q * 3 + 1)
                    e.reciprocal(rec, den[:, i % 2]).then_inc(s_ls, 1)
                    e.wait_ge(s_ls, START + q * 3 + 2)
                    e.tensor_tensor(ratio[:, i % 2], l1_num(i)[:, 0:C], rec, ALU.mult).then_inc(s_ls, 1)

                l1_norm(0, 0)

                def l1_slot(t, u, i, stages=3, last=False):
                    g = at_(e, gb + t)
                    if stages > 2:
                        g2 = g if i >= 2 else e.snap(g - 1)
                        l1_ratio(e.snap(g * SUBS + i - 2), g2, (i - 2) % SUBS)
                    if i == 1 and not last:
                        e.wait_ge(s_lt, START + g * SUBS)
                        l1_norm(t + 1, 1 - u)

                walk_layer1(e, l1_slot)
                l1_ratio(e.snap(end * SUBS - 2), last, SUBS - 2)
                l1_ratio(e.snap(end * SUBS - 1), last, SUBS - 1)


def layout(x, w_in, w_conv, b_conv, dt_bias, a_log, d_param, gamma, beta, w_out):
    f = np.float32

    def by_partition(a, k):
        return np.ascontiguousarray(np.moveaxis(a.reshape(k, P, *a.shape[1:]), 0, 1))

    xbc = np.zeros((C, XC * P), f)
    xbc[:, 0:DI + NS] = w_in[:, DI:2 * DI + NS]
    xbc[:, DI + C_AT:DI + C_AT + NS] = w_in[:, 2 * DI + NS:2 * DI + 2 * NS]
    wc, bc = np.zeros((XC * P, TAPS), f), np.zeros((XC * P,), f)
    taps = w_conv.reshape(TAPS, -1).T
    wc[0:DI + NS], bc[0:DI + NS] = taps[0:DI + NS], b_conv[0:DI + NS]
    at = DI + C_AT
    wc[at:at + NS], bc[at:at + NS] = taps[DI + NS:], b_conv[DI + NS:]
    chan = np.stack([gamma.reshape(ZC, P), beta.reshape(ZC, P), np.repeat(d_param, HD).reshape(ZC, P)])
    k, m = np.arange(P)[:, None], np.arange(P)[None, :]
    ch, grp = np.arange(C), np.arange(GROUPS)
    to_group = (ch[:, None] // GC == grp[None, :]).astype(f)
    lo, hi = WIN_W // 2, WIN_W - WIN_W // 2 - 1
    band_w = ((k // W == m // W) & (k >= m - lo) & (k <= m + hi)).astype(f)
    count = band_w.sum(0, keepdims=True)
    lo, hi = WIN_C // 2, WIN_C - WIN_C // 2 - 1
    band = ((ch[:, None] >= ch[None, :] - lo) & (ch[:, None] <= ch[None, :] + hi)).astype(f)
    band_c = np.zeros((P, KC, BANDC), f)
    for n in range(KC):
        band_c[:, n, 0:BAND_HI[n] - BAND_LO[n]] = band[n * P:(n + 1) * P, BAND_LO[n]:BAND_HI[n]]
    xt = x.reshape(NB * TILES, TT, KC, P).transpose(0, 3, 2, 1)
    return {
        "x": np.ascontiguousarray(xt),
        "w_xbc": by_partition(xbc, KC), "w_z": by_partition(w_in[:, 0:DI], KC),
        "w_dt": by_partition(w_in[:, 2 * DI + 2 * NS:], KC), "w_out": by_partition(w_out, ZC),
        "w_conv": by_partition(wc, XC), "b_conv": by_partition(bc, XC),
        "chan": np.ascontiguousarray(chan.transpose(2, 0, 1)),
        "dt_bias": np.tile(dt_bias, (P, 1)), "neg_a": np.tile(a_log, (P, 1)),
        "upto": (k <= m).astype(f), "after": (k > m).astype(f), "ones": np.ones((P, P), f),
        "ident": np.eye(P, dtype=f), "to_group": by_partition(to_group, KC),
        "from_group": np.ascontiguousarray(to_group.T), "band_w": band_w, "band_wn": band_w * count, "band_c": band_c,
    }


def kernel(x, L0_conv_W_in, L0_conv_W_conv, L0_conv_b_conv, L0_conv_dt_bias, L0_conv_A_log, L0_conv_D_param,
           L0_conv_gamma, L0_conv_beta, L0_conv_W_out):
    import concourse.bacc as bacc
    from concourse.bass_utils import run_bass_kernel_spmd

    arrays = layout(*(np.asarray(v) for v in (
        x, L0_conv_W_in, L0_conv_W_conv, L0_conv_b_conv, L0_conv_dt_bias, L0_conv_A_log, L0_conv_D_param,
        L0_conv_gamma, L0_conv_beta, L0_conv_W_out)))
    nc = bacc.Bacc("TRN2", target_bir_lowering=False, num_devices=1)
    aps = {n: nc.dram_tensor(f"in_{n}", a.shape, mybir.dt.from_np(a.dtype), kind="ExternalInput").ap()
           for n, a in arrays.items()}
    aps["out"] = nc.dram_tensor("out", (NB * TILES, TT, C), F32, kind="ExternalOutput").ap()
    build(nc, aps)
    r = run_bass_kernel_spmd(nc, [{f"in_{n}": a for n, a in arrays.items()}], core_ids=[0])
    return r.results[0]["out"].reshape(NB, H, W, C)
```

```python
from contextlib import ExitStack

import numpy as np

import concourse.bass as bass
from concourse import mybir

F32 = mybir.dt.float32
F32R = mybir.dt.float32r
ALU = mybir.AluOpType
ACT = mybir.ActivationFunctionType

P = 128
NB, H, W, C = 8, 64, 64, 384
KC = C // P
HEADS, HD, NS = 12, 64, 16
DI = HEADS * HD
ZC = DI // P
XC = ZC + 1
C_AT = 32
AT1, AT2 = 32, 64
STACK = AT2 + NS
ROWS = 8
TT = ROWS * W
TILES = H // ROWS
SUBS = TT // P
NSUB = TILES * SUBS
HG = 4
NG = HEADS // HG
HB = DI // 2
TAPS = 9
PAIRS = (XC + 1) // 2
TPP = 2 * TAPS
TPT = PAIRS * TPP
CONV_CUTS = [(0, 8, 14, TPP), (10, 14, 16, TPP), (2, 8, 14, TPP), (0, 12, TPP, TPP)]
MIDDLE = [(0,), (0,), (0,), (0,)]
LATE = [(1,), (1,), (1,), (1,)]
LAST = [(2,), (), (2,), ()]
SPT = XC + 1
GROUPS = 32
GC = C // GROUPS
WIN_W, WIN_C = 5, 20
HALF = TT // 2
EPS = 1e-5
LOG_TERMS = 8
NORMS = 2 * KC
SP_STEPS = 12 + LOG_TERMS
GN_STEPS = 10
FIRST_POOL = (2, 3)
FIRST_STEPS = len(FIRST_POOL) * (2 * TAPS - 1)
START = 4
TINY = float(np.finfo(np.float32).tiny)
AHEAD = WIN_C - WIN_C // 2 - 1
BAND_LO = [0, P - AHEAD, 2 * P - AHEAD]
BAND_HI = [P + WIN_C // 2, 2 * P + WIN_C // 2, C]
BANDC = max(h - l for l, h in zip(BAND_LO, BAND_HI))
CONSTS = ["w_xbc", "w_z", "w_dt", "w_out", "w_conv", "b_conv", "chan", "d_heads", "dt_bias", "neg_a", "upto", "after", "ones",
          "ident", "to_group", "from_group", "band_w", "band_wn", "band_c"]
IN_PROJ = [(1, (2, 3)), (1, (4, 5)), (1, (6,)), (2, (0, 1))]


def at_(e, v):
    return v if isinstance(v, int) else e.snap(v)


def walk_scan(e, gb, slot):
    slot(0, 0, 0, first=True, top=True)
    slot(0, 0, 1, top=True)
    slot(0, 0, 2, top=True)
    with e.Fori(0, TILES // 2 - 1) as pair:
        t0 = e.snap(pair * 2)
        for k in range(3, 2 * SUBS + 3):
            slot(e.snap(t0 + k // SUBS), (k // SUBS) % 2, k % SUBS)
    for k in range(3, 2 * SUBS):
        t = TILES - 2 + k // SUBS
        slot(t, t % 2, k % SUBS, left=TILES - 1 - t)


def walk_layer1(e, slot):
    for i in range(SUBS):
        slot(0, 0, i, stages=min(i + 1, 3))
    with e.Fori(0, TILES // 2 - 1) as pair:
        for u in (1, 0):
            t = e.snap(pair * 2 + 2 - u)
            for i in range(SUBS):
                slot(t, u, i)
    for i in range(SUBS):
        slot(TILES - 1, 1, i, last=True)


def build(nc, A):
    with ExitStack() as ctx:
        def sb(name, *shape, dtype=F32):
            return ctx.enter_context(nc.sbuf_tensor(name, list(shape), dtype))

        def sem(name):
            return ctx.enter_context(nc.semaphore(name))

        w_xbc = sb("w_xbc", P, KC, XC * P)
        w_z = sb("w_z", P, KC, DI)
        w_dt = sb("w_dt", P, KC, HEADS)
        w_out = sb("w_out", P, ZC, C)
        w_conv = sb("w_conv", P, XC, TAPS)
        b_conv = sb("b_conv", P, XC)
        chan = sb("chan", P, 2, ZC)
        d_heads = sb("d_heads", P, HEADS)
        dt_bias = sb("dt_bias", P, HEADS)
        neg_a = sb("neg_a", P, HEADS)
        upto = sb("upto", P, P)
        after = sb("after", P, P)
        ones = sb("ones", P, P)
        ident = sb("ident", P, P)
        to_group = sb("to_group", P, KC, GROUPS)
        from_group = sb("from_group", GROUPS, C)
        band_w = sb("band_w", P, P)
        band_wn = sb("band_wn", P, P)
        band_c = sb("band_c", P, KC, BANDC)
        minus_half = sb("minus_half", P, KC)
        after_r = sb("after_r", P, P, dtype=F32R)

        xb = sb("xb", P, KC, (H + 1) * W)
        stats = sb("stats", P, KC, 2 * TILES, 6)
        mean_var = sb("mean_var", P, KC, 2)
        g_mean = sb("g_mean", P, KC)
        g_tmp = sb("g_tmp", P, KC)
        g_var = sb("g_var", P, KC)
        g_rstd = sb("g_rstd", P, KC)
        g_red = sb("g_red", GROUPS, 2)
        dt = sb("dt", P, NSUB * HEADS)
        e_from = sb("e_from", P, NSUB * HEADS)
        e_to = sb("e_to", P, NSUB * HEADS)
        e_all = sb("e_all", P, NSUB * HEADS)
        a_hi = sb("a_hi", P, NSUB * HEADS, dtype=F32R)
        a_lo = sb("a_lo", P, NSUB * HEADS)

        cb = sb("cb", P, XC, ROWS + 2, W + 2)
        xs = sb("xs", P, 2, XC, TT)
        ct = sb("ct", NS, 2, TT)
        gate = sb("gate", P, 2, ZC, HALF)
        xres = sb("xres", P, 2, KC, HALF)

        a_tri = sb("a_tri", P, NG, 2, HG * P, dtype=F32R)
        mix = sb("mix", P, NG, HG * P)
        bc_m = sb("bc_m", P, P)
        b_tok = sb("b_tok", P, 2, NS)
        x_tok = sb("x_tok", P, DI)
        xd = sb("xd", P, 2, DI)
        x_dt, x_end = xd[:, 0], xd[:, 1]
        y = sb("y", P, DI)
        sp0, sp1, sp2 = a_lo, y[:, 0:NSUB * HEADS], y[:, NSUB * HEADS:2 * NSUB * HEADS]
        state = sb("state", NS, DI)
        c_st = sb("c_st", STACK, 2, TT, dtype=F32R)
        state_st = sb("state_st", STACK, DI, dtype=F32R)
        ln_st = sb("ln_st", P, 2, 6)
        ln_mv = sb("ln_mv", P, 2)
        ln_vm = sb("ln_vm", P, 2)
        ln_rs = sb("ln_rs", P, 2)
        aff = sb("aff", P, ZC, P)
        y_in = aff[:].rearrange("p c n -> p (c n)")
        a_dt = aff[:].rearrange("p c n -> p (c n)")[:, 0:NSUB * HEADS]

        gate_flat = gate[:].rearrange("p h c n -> p (h c n)")
        xg = [xd[:].rearrange("p u c -> p (u c)").rearrange("p (k n) -> p k n", k=KC),
              gate_flat[:, SUBS * C:].rearrange("p (k n) -> p k n", k=KC)]
        x1c = mix[:, :, :]
        out_b = gate_flat[:, 0:SUBS * C].rearrange("p (s c) -> p s c", s=SUBS)
        xs_flat = xs[:].rearrange("p u c n -> p (u c n)")

        def dt_rows(n):
            return xs[0:HEADS, 1, n % 4]

        def carve(n):
            return xs_flat[:, n * 2 * C:(n + 1) * 2 * C].rearrange("p (n c) -> p n c", n=2)

        xg_t, sq_t, s2, qw, den, ratio, x1_t = (carve(n) for n in range(7))
        rec, total, no_den = carve(7)[:, 0], carve(7)[:, 1], carve(8)[:, 0]

        pb = [ctx.enter_context(nc.psum_tensor(f"proj{i}", [P, 512], F32)) for i in range(2)]
        tr = ctx.enter_context(nc.psum_tensor("tr", [P, 2, 512], F32))
        ring = [ctx.enter_context(nc.psum_tensor(f"ring{i}", [P, 512], F32)) for i in range(2)]
        yp = ctx.enter_context(nc.psum_tensor("yp", [P, 2, 512], F32))


        def l1_num(i):
            return ring[0][:] if i % 2 == 0 else yp[:, 0]

        def l1_den(i):
            return ring[1][:] if i % 2 == 0 else yp[:, 1]

        s_const, s_setup = sem("consts_loaded"), sem("setup_done")
        s_half, s_expa = sem("minus_half_ready"), sem("exp_a_ready")
        s_x = sem("x_loaded")
        s_res = [sem(f"residual_loaded{h}") for h in range(2)]
        s_out = [sem(f"out_stored{i}") for i in range(SUBS)]
        s_xst = sem("x_stats")
        s_gp, s_gv, s_gr = sem("gn_summed"), sem("gn_step"), sem("gn_rstd")
        s_norm, s_zero = sem("x_normalised"), sem("image_zeroed")
        s_dtm, s_dtc = sem("dt_rows_projected"), sem("dt_rows_stored")
        s_dtp, s_sp, s_dte, s_sum, s_exps = (
            sem(n) for n in ("dt_transposed", "softplus_step", "dt_exp", "a_summed", "decays_ready"))
        s_r0p, s_r0 = sem("row0_projected"), sem("row0_stored")
        s_xbc, s_ev = sem("xbc_projected"), sem("xbc_stored")
        s_tap, s_silu = sem("conv_tap"), sem("silu_done")
        s_z, s_zev = sem("z_projected"), sem("z_stored")
        s_op, s_oev = sem("out_projected"), sem("out_added")
        s_x1st = sem("x1_stats")
        s_xt, s_xtr = sem("x_transposed"), sem("x_transposed_read")
        s_ch, s_cl, s_sh, s_sl = sem("c_hi_ready"), sem("c_lo_ready"), sem("state_hi_ready"), sem("state_lo_ready")
        s_xc, s_xdt, s_dx, s_yi = sem("x_copied"), sem("x_dt_ready"), sem("d_x_ready"), sem("y_terms_added")
        s_at, s_d, s_e, s_m = sem("a_tri_ready"), sem("decay_summed"), sem("decay_ready"), sem("mix_ready")
        s_y, s_yoff, s_t1 = sem("y_summed"), sem("y_of_state"), sem("y_of_state_read")
        s_xe, s_sn, s_ss, s_sa = sem("x_end_ready"), sem("state_product"), sem("state_scaled"), sem("state_added")
        s_yr, s_yst, s_var, s_rs, s_yn = sem("y_ready"), sem("y_stats"), sem("y_var"), sem("y_rstd"), sem("y_normed")
        s_ynt, s_aff, s_g = sem("y_transposed"), sem("y_scaled"), sem("gated")
        s_lx, s_lc = sem("l1_x_ready"), sem("l1_copy_ready")
        s_lt, s_la, s_lw, s_lb, s_lq = (
            sem(n) for n in ("l1_transposed", "l1_squares", "l1_box_w", "l1_box_read", "l1_box_c"))
        s_ls, s_lr, s_lbase, s_lo = sem("l1_step"), sem("l1_x1_read"), sem("l1_terms"), sem("l1_out")
        s_first = sem("conv_first_tile_step")

        block = ctx.enter_context(nc.Block())

        @block.sync
        def _(e):
            for counted in (*s_out,):
                e.sem_inc(counted, START)
            bufs = dict(w_xbc=w_xbc, w_z=w_z, w_dt=w_dt, w_out=w_out, w_conv=w_conv, b_conv=b_conv, chan=chan, d_heads=d_heads,
                        dt_bias=dt_bias, neg_a=neg_a, upto=upto, after=after, ones=ones, ident=ident,
                        to_group=to_group, from_group=from_group, band_w=band_w, band_wn=band_wn, band_c=band_c)
            for name in CONSTS:
                e.dma_start(bufs[name][:], A[name]).then_inc(s_const, 16)

            def load(g, t):
                at = t * TT if isinstance(t, int) else e.snap(t * TT)
                e.dma_start(xb[:, :, bass.ds(at, TT)], A["x"][bass.ds(g, 1)].rearrange("g p k n -> (g p) k n")
                            ).then_inc(s_x, 16)

            def image(gb, more):
                def slot(t, u, i, first=False, top=False, left=TILES):
                    g = at_(e, gb + t)
                    if i % 2 == 1:
                        e.wait_ge(s_xtr, START + g * SUBS + i + 1)
                        h = i // 2
                        e.dma_start(xres[:, h], A["x"][bass.ds(g, 1), :, :, h * HALF:(h + 1) * HALF]
                                    .rearrange("g p k n -> (g p) k n")).then_inc(s_res[h], 16)

                walk_scan(e, gb, slot)
                with e.Fori(0, TILES) as t:
                    g = at_(e, gb + t)
                    if more:
                        e.wait_ge(s_lx, START + g + 1)
                        e.wait_ge(s_lc, START + g + 1)
                        load(e.snap(g + TILES), t)
                    for i in range(SUBS):
                        e.wait_ge(s_lo, START + g * SUBS + i + 1)
                        e.dma_start(A["out"][bass.ds(g, 1), i * P:(i + 1) * P].rearrange("g p c -> (g p) c"),
                                    out_b[:, i]).then_inc(s_out[i], 16)

            for t in range(TILES):
                load(t, t)
            if NB > 1:
                with e.Fori(0, NB - 1) as b:
                    image(e.snap(b * TILES), True)
            image((NB - 1) * TILES, False)
            for i in range(SUBS):
                e.wait_ge(s_out[i], START + 16 * NB * TILES)

        @block.gpsimd
        def _(e):
            for counted in (s_xe, s_rs, s_lo, s_yi):
                e.sem_inc(counted, START)
            e.memset(minus_half[:], -0.5).then_inc(s_half, 1)
            e.wait_ge(s_half, 1)

            def root(n):
                e.wait_ge(s_gv, n * GN_STEPS + GN_STEPS)
                e.tensor_tensor(g_rstd[:], g_var[:], minus_half[:], ALU.pow).then_inc(s_gr, 1)

            def ln_root(sp):
                e.wait_ge(s_var, sp + 1)
                e.wait_ge(s_yn, START + sp)
                e.tensor_tensor(ln_rs[:, 0:1], ln_vm[:, 0:1], minus_half[:, 0:1], ALU.pow).then_inc(s_rs, 1)
                e.wait_ge(s_rs, START + sp * 2 + 1)
                e.tensor_tensor(ln_rs[:, 1:2], ln_vm[:, 1:2], ln_rs[:, 0:1], ALU.mult).then_inc(s_rs, 1)

            def add_dx(sp):
                e.wait_ge(s_t1, sp * 2 + 2)
                e.wait_ge(s_dx, sp + 1)
                e.tensor_tensor(y_in, y_in, x_tok[:], ALU.add).then_inc(s_yi, 1)

            e.wait_ge(s_const, 16 * len(CONSTS))
            with e.Fori(0, NB) as b:
                gb = e.snap(b * TILES)
                root(e.snap(b * 2))
                e.wait_ge(s_lo, START + gb * SUBS)
                e.wait_ge(s_r0, b + 1)
                product = x_end[:, 0:TT].rearrange("p (r w) -> p r w", w=W)
                steps = [0]

                def first_step(ins):
                    steps[0] += 1
                    ins.then_inc(s_first, 1)
                    e.wait_ge(s_first, b * FIRST_STEPS + steps[0])

                for c in FIRST_POOL:
                    e.wait_ge(s_ev, START + (gb * XC + c + 1) * 2)
                    acc = xs[:, 0, c].rearrange("p (r w) -> p r w", w=W)
                    for tap in range(TAPS):
                        src = cb[:, c, tap // 3:ROWS + tap // 3, tap % 3:tap % 3 + W]
                        weight = w_conv[:, c, tap:tap + 1].unsqueeze(2).to_broadcast([P, ROWS, W])
                        first_step(e.tensor_tensor(product if tap else acc, src, weight, ALU.mult))
                        if tap:
                            first_step(e.tensor_tensor(acc, acc, product, ALU.add))
                assert steps[0] == FIRST_STEPS, steps
                e.wait_ge(s_sp, (b + 1) * SP_STEPS)
                e.wait_ge(s_exps, b * 3 + 3)

                def slot(t, u, i, first=False, top=False, left=TILES):
                    g = at_(e, gb + t)
                    s = e.snap(g * SUBS + i)
                    at = e.snap((t * SUBS + i) * HEADS) if not isinstance(t, int) else (t * SUBS + i) * HEADS
                    e.wait_ge(s_d, START + s * NG)
                    for j in range(NG):
                        for part, src in enumerate((a_hi[:].bitcast(F32), a_lo[:])):
                            a = src[:, bass.ds(at + j * HG, HG)]
                            e.tensor_tensor(a_tri[:, j, part].rearrange("p (h l) -> p h l", h=HG),
                                            a.unsqueeze(2).to_broadcast([P, HG, P]),
                                            upto[:].unsqueeze(1).to_broadcast([P, HG, P]), ALU.mult).then_inc(s_at, 1)
                        if j == 0 and not first:
                            add_dx(e.snap(s - 1))
                        if j == 1 and not first:
                            ln_root(e.snap(s - 1))

                    def by_head(out, in_, factor):
                        return e.tensor_tensor(out.rearrange("p (h d) -> p h d", h=HEADS),
                                               in_.rearrange("p (h d) -> p h d", h=HEADS),
                                               factor.unsqueeze(2).to_broadcast([P, HEADS, HD]), ALU.mult)

                    e.wait_ge(s_xc, s + 1)
                    e.wait_ge(s_y, START + s)
                    e.wait_ge(s_xe, START + s)
                    by_head(x_dt, x_tok[:], dt[:, bass.ds(at, HEADS)]).then_inc(s_xdt, 1)
                    e.wait_ge(s_xdt, s + 1)
                    e.wait_ge(s_sn, START + s * 2)
                    by_head(x_end, x_dt, e_to[:, bass.ds(at, HEADS)]).then_inc(s_xe, 1)
                    by_head(x_tok[:], x_tok[:], d_heads[:]).then_inc(s_dx, 1)
                    e.wait_ge(s_sh, s + 1)
                    part = state_st[0:NS].bitcast(F32)
                    e.tensor_tensor(state_st[0:NS], state[:], part, ALU.subtract).then_inc(s_sl, 1)
                    e.wait_ge(s_sl, s + 1)
                    sv = state[:].rearrange("p (h d) -> p h d", h=HEADS)
                    e.tensor_tensor(sv, sv, e_all[0:NS, bass.ds(at, HEADS)].unsqueeze(2).to_broadcast([NS, HEADS, HD]),
                                    ALU.mult).then_inc(s_ss, 1)

                walk_scan(e, gb, slot)
                add_dx(e.snap((gb + TILES) * SUBS - 1))
                ln_root(e.snap((gb + TILES) * SUBS - 1))
                root(e.snap(b * 2 + 1))

                def l1_add(q, g, i):
                    e.wait_ge(s_ls, START + q * 3 + 3)
                    e.wait_ge(s_lr, START + q + 1)
                    e.wait_ge(s_lo, START + q)
                    e.tensor_tensor(total, ratio[:, i % 2], x1_t[:, i % 2], ALU.add).then_inc(s_lbase, 1)
                    e.tensor_scalar(no_den, den[:, i % 2], TINY, None, ALU.is_le).then_inc(s_lbase, 1)
                    e.wait_ge(s_out[i], START + g * 16)
                    e.wait_ge(s_lbase, q * 2 + 2)
                    e.tensor_tensor(out_b[:, i], total, no_den, ALU.add).then_inc(s_lo, 1)

                def l1_slot(t, u, i, stages=3, last=False):
                    if stages > 2:
                        g = at_(e, gb + t)
                        l1_add(e.snap(g * SUBS + i - 2), g if i >= 2 else e.snap(g - 1), (i - 2) % SUBS)

                walk_layer1(e, l1_slot)
                end = e.snap(gb + TILES)
                for i in (SUBS - 2, SUBS - 1):
                    l1_add(e.snap((end - 1) * SUBS + i), e.snap(end - 1), i)

        @block.tensor
        def _(e):
            for counted in (s_d, s_sn, s_y, s_yoff, s_ynt, s_op, s_lq, s_lt):
                e.sem_inc(counted, START)
            def gn_sums(n):
                for r, ready in enumerate((3, 8)):
                    e.wait_ge(s_gv, n * GN_STEPS + ready)
                    for k in range(KC):
                        src = mean_var[:, k, 0:1] if r == 0 else g_tmp[:, k:k + 1]
                        mm = e.matmul(yp[0:GROUPS, 0, r:r + 1], to_group[:, k], src, start=(k == 0), stop=(k == KC - 1))
                    mm.then_inc(s_gp, 1)
                    e.wait_ge(s_gv, n * GN_STEPS + ready + 1)
                    for k in range(KC):
                        mm = e.matmul(yp[:, 1, KC * r + k:KC * r + k + 1], from_group[:, k * P:(k + 1) * P],
                                      g_red[:, r:r + 1], start=True, stop=True)
                    mm.then_inc(s_gp, 1)

            def in_proj(gx, tx, c):
                e.wait_ge(s_ev, START + (gx * XC + c) * 2)
                for k in range(KC):
                    mm = e.matmul(pb[0][:], w_xbc[:, k, c * P:(c + 1) * P], xb[:, k, bass.ds(tx * TT + W, TT)],
                                  start=(k == 0), stop=(k == KC - 1))
                mm.then_inc(s_xbc, 1)

            def z_proj(gx, tx, h, q, outs):
                e.wait_ge(s_zev, START + gx * 6 + h * 3 + q)
                e.wait_ge(s_oev, START + outs)
                for c in range(2):
                    for k in range(KC):
                        mm = e.matmul(pb[1][:, c * HALF:(c + 1) * HALF], w_z[:, k, (2 * q + c) * P:(2 * q + c + 1) * P],
                                      xb[:, k, bass.ds(tx * TT + h * HALF, HALF)], start=(k == 0), stop=(k == KC - 1))
                mm.then_inc(s_z, 1)

            def out_proj(gx, h, q, gated, zs):
                e.wait_ge(s_g, START + gated)
                e.wait_ge(s_zev, START + zs)
                e.wait_ge(s_oev, START + gx * 4 + h * 2 + q)
                for n, m in enumerate(((0, 1), (2,))[q]):
                    for k in range(ZC):
                        mm = e.matmul(pb[1][:, n * HALF:(n + 1) * HALF], w_out[:, k, m * P:(m + 1) * P], gate[:, h, k],
                                      start=(k == 0), stop=(k == ZC - 1))
                mm.then_inc(s_op, 1)

            def y_transpose(sp):
                e.wait_ge(s_yn, START + sp + 1)
                for c in range(ZC):
                    mm = e.transpose(tr[:, c // KC, (c % KC) * P:(c % KC + 1) * P], y[:, c * P:(c + 1) * P], ident[:])
                mm.then_inc(s_ynt, 1)

            e.wait_ge(s_const, 16 * len(CONSTS))
            with e.Fori(0, NB) as b:
                gb = e.snap(b * TILES)
                gn_sums(e.snap(b * 2))
                e.wait_ge(s_norm, b * NORMS + KC)
                e.wait_ge(s_zero, b + 1)
                for c in range(XC):
                    for k in range(KC):
                        mm = e.matmul(tr[:, 0, c * W:(c + 1) * W], w_xbc[:, k, c * P:(c + 1) * P], xb[:, k, 0:W],
                                      start=(k == 0), stop=(k == KC - 1))
                mm.then_inc(s_r0p, 1)
                for c in range(ZC):
                    in_proj(gb, 0, c)
                e.wait_ge(s_norm, (b + 1) * NORMS)

                def dt_transpose(n):
                    for i in range(SUBS):
                        at = (n * SUBS + i) * HEADS
                        mm = e.transpose(tr[:, 1, at:at + HEADS], dt_rows(n)[:, i * P:(i + 1) * P],
                                         ident[0:HEADS, 0:HEADS])
                    mm.then_inc(s_dtp, 1)

                for n in range(TILES):
                    for k in range(KC):
                        if k == 1 and n:
                            e.wait_ge(s_dtc, b * TILES + n)
                        mm = e.matmul(yp[0:HEADS, n % 2], w_dt[:, k], xb[:, k, n * TT:(n + 1) * TT],
                                      start=(k == 0), stop=(k == KC - 1))
                    mm.then_inc(s_dtm, 1)
                    if n:
                        dt_transpose(n - 1)
                e.wait_ge(s_dtc, (b + 1) * TILES)
                in_proj(gb, 0, ZC)
                dt_transpose(TILES - 1)
                for c in range(2):
                    in_proj(e.snap(gb + 1), 1, c)
                e.wait_ge(s_sp, (b + 1) * SP_STEPS - 2)
                for mask, bank in ((upto, yp[:, 0]), (after, yp[:, 1]), (ones, ring[0][:])):
                    e.matmul(bank[:, 0:NSUB * HEADS], mask[:], a_dt, start=True, stop=True).then_inc(s_sum, 1)

                def slot(t, u, i, first=False, top=False, left=TILES):
                    g = at_(e, gb + t)
                    s = e.snap(g * SUBS + i)
                    tok = slice(i * P, (i + 1) * P)
                    off, chunks = IN_PROJ[i]
                    chunks = chunks if off <= left else ()

                    def filler(qs):
                        for q in qs:
                            if i % 2 == 0:
                                z_proj(g, t, i // 2, q, g * 4 if i or top else e.snap(g * 4 - 2))
                            elif i == 3:
                                out_proj(g, 0, q, s - 1, g * 6 + 6)
                            elif not top:
                                out_proj(e.snap(g - 1), 1, q, s - 1, g * 6 + 3)

                    e.wait_ge(s_silu, (g + 1) * SPT)
                    e.wait_ge(s_xtr, START + s)
                    if first:
                        e.wait_ge(s_r0, b + 1)
                        e.wait_ge(s_exps, b * 3 + 3)
                    else:
                        e.wait_ge(s_aff, START + s - 1)
                    for c in range(ZC):
                        e.transpose(tr[:, c // KC, (c % KC) * P:(c % KC + 1) * P], xs[:, u, c, tok], ident[:])
                    e.transpose(tr[:, 1, HB:HB + NS], xs[0:NS, u, ZC, tok], ident[0:NS, 0:NS])
                    e.matmul(tr[:, 0, HB:HB + P], xs[0:NS, u, ZC, tok], ct[:, u, tok],
                             start=True, stop=True).then_inc(s_xt, 1)
                    if chunks:
                        in_proj(e.snap(g + off), e.snap(t + off), chunks[0])
                    for j in range(NG):
                        if j == 0:
                            e.wait_ge(s_sa, START + s * 2)
                        if j == 2:
                            if not first:
                                e.wait_ge(s_xc, s + 1)
                                e.wait_ge(s_xtr, START + s + 1)
                                y_transpose(e.snap(s - 1))
                            e.wait_ge(s_e, s * NG + 1)
                        e.wait_ge(s_at, (s * NG + j) * 2 + 2)
                        for part in range(2):
                            mm = e.matmul(ring[j % 2][:], after_r[:], a_tri[:, j, part], start=(part == 0),
                                          stop=(part == 1))
                        mm.then_inc(s_d, 1)
                    filler(MIDDLE[i])
                    if len(chunks) > 1:
                        in_proj(e.snap(g + off), e.snap(t + off), chunks[1])
                    e.wait_ge(s_yr, START + s)
                    e.wait_ge(s_xdt, s + 1)
                    for h in range(HEADS):
                        if h % HG == 0:
                            e.wait_ge(s_m, s * NG + h // HG + 1)
                        at = (h % (HEADS // 2)) * HD
                        mm = e.matmul(yp[:, h // (HEADS // 2), at:at + HD],
                                      mix[:, h // HG, (h % HG) * P:(h % HG + 1) * P],
                                      x_dt[:, h * HD:(h + 1) * HD], start=(h % (HEADS // 2) == 0),
                                      stop=(h % (HEADS // 2) == HEADS // 2 - 1), skip_group_check=True)
                    mm.then_inc(s_y, 1)
                    if i == 0:
                        e.wait_ge(s_cl, g + 1)
                    e.wait_ge(s_sl, s + 1)
                    for n in range(2):
                        e.wait_ge(s_e, s * NG + n + 2)
                        e.matmul(ring[1 - n][:, 0:HB], c_st[:, u, tok], state_st[:, n * HB:(n + 1) * HB],
                                 start=True, stop=True).then_inc(s_yoff, 1)
                    filler(LATE[i])
                    e.wait_ge(s_xe, START + s + 1)
                    for n in range(2):
                        e.wait_ge(s_t1, s * 2 + n + 1)
                        e.matmul(ring[1 - n][0:NS, 0:HB], b_tok[:, i % 2], x_end[:, n * HB:(n + 1) * HB],
                                 start=True, stop=True).then_inc(s_sn, 1)
                    filler(LAST[i])

                walk_scan(e, gb, slot)
                end = e.snap(gb + TILES)
                y_transpose(e.snap(end * SUBS - 1))
                for q in range(2):
                    out_proj(e.snap(end - 1), 1, q, end * SUBS, end * 6)

                gn_sums(e.snap(b * 2 + 1))

                def l1_stage1(q, u, i):
                    e.wait_ge(s_la, START + q * 2)
                    for k in range(KC):
                        mm = e.transpose(pb[0][:, k * P:(k + 1) * P], xg[u][:, k, i * P:(i + 1) * P], ident[:])
                    mm.then_inc(s_lt, 1)

                def l1_stage2(q, i):
                    e.wait_ge(s_la, START + q * 2 + 2)
                    e.wait_ge(s_lb, START + q * 2)
                    for src, band, n in ((xg_t, band_w, 0), (sq_t, band_wn, 1)):
                        for k in range(KC):
                            mm = e.matmul(tr[:, n, k * P:(k + 1) * P], src[:, i % 2, k * P:(k + 1) * P], band[:],
                                          start=True, stop=True)
                    mm.then_inc(s_lw, 1)

                def l1_stage3(q, i):
                    e.wait_ge(s_lb, START + q * 2 + 2)
                    e.wait_ge(s_ls, START + q * 3 - 3)
                    for src, bank in ((qw, l1_den(i)), (s2, l1_num(i))):
                        for k in range(KC):
                            mm = e.matmul(bank[:, BAND_LO[k]:BAND_HI[k]], src[:, i % 2, k * P:(k + 1) * P],
                                          band_c[:, k, 0:BAND_HI[k] - BAND_LO[k]], start=(k == 0), stop=(k == KC - 1),
                                          skip_group_check=True)
                    e.wait_ge(s_lr, START + q)
                    for k in range(KC):
                        mm = e.transpose(pb[1][:, k * P:(k + 1) * P], x1c[:, k, i * P:(i + 1) * P], ident[:])
                    mm.then_inc(s_lq, 1)

                def l1_slot(t, u, i, stages=3, last=False):
                    g = at_(e, gb + t)
                    q = e.snap(g * SUBS + i)
                    if i == 0:
                        e.wait_ge(s_lx, START + g + 1)
                    l1_stage1(q, u, i)
                    if stages > 1:
                        l1_stage2(e.snap(q - 1), (i - 1) % SUBS)
                    if stages > 2:
                        if i == 2:
                            e.wait_ge(s_lc, START + g + 1)
                        l1_stage3(e.snap(q - 2), (i - 2) % SUBS)

                walk_layer1(e, l1_slot)
                q = e.snap(end * SUBS)
                l1_stage2(e.snap(q - 1), SUBS - 1)
                l1_stage3(e.snap(q - 2), SUBS - 2)
                l1_stage3(e.snap(q - 1), SUBS - 1)

        @block.scalar
        def _(e):
            for counted in (s_lc, s_yn, s_ev, s_zev, s_aff, s_la, s_lb, s_lr):
                e.sem_inc(counted, START)
            def act(out, in_, func, **kw):
                return e.activation(out, in_, func, **kw)

            def store_xbc(gx, c, halo):
                if halo:
                    e.wait_ge(s_tap, (gx - 1) * TPT + (c // 2 + 1) * TPP)
                    act(cb[:, c, 0:2, :], cb[:, c, ROWS:ROWS + 2, :], ACT.Copy).then_inc(s_ev, 1)
                    e.wait_ge(s_ev, START + (gx * XC + c) * 2 + 1)
                e.wait_ge(s_xbc, gx * XC + c + 1)
                act(cb[:, c, 2:ROWS + 2, 1:W + 1], pb[0][:].rearrange("p (r w) -> p r w", w=W), ACT.Copy
                    ).then_inc(s_ev, 1 if halo else 2)

            def silu(gx, u, c):
                e.wait_ge(s_tap, gx * TPT + (c // 2 + 1) * TPP)
                if c < ZC:
                    act(xs[:, u, c], xs[:, u, c], ACT.Silu, bias=b_conv[:, c:c + 1]).then_inc(s_silu, 1)
                else:
                    act(ct[:, u], xs[C_AT:C_AT + NS, u, c], ACT.Silu, bias=b_conv[C_AT:C_AT + NS, c:c + 1]).then_inc(s_silu, 1)
                    act(xs[0:NS, u, c], xs[0:NS, u, c], ACT.Silu, bias=b_conv[0:NS, c:c + 1]).then_inc(s_silu, 1)
                    e.wait_ge(s_silu, (gx + 1) * SPT - 1)
                    for lo in (0, AT1):
                        a = act(c_st[lo:lo + NS, u], ct[:, u], ACT.Copy)
                    a.then_inc(s_ch, 1)

            def silu_z(gx, h, q, free):
                e.wait_ge(s_op, START + free)
                e.wait_ge(s_z, gx * 6 + h * 3 + q + 1)
                act(gate[:, h, 2 * q:2 * q + 2].rearrange("p c n -> p (c n)"), pb[1][:], ACT.Silu).then_inc(s_zev, 1)

            def y_norm(sp):
                e.wait_ge(s_rs, START + sp * 2 + 2)
                act(y[:], y[:], ACT.Identity, bias=ln_rs[:, 1:2], scale=ln_rs[:, 0:1]).then_inc(s_yn, 1)

            def y_scale(sp):
                e.wait_ge(s_ynt, START + sp + 1)
                e.wait_ge(s_g, START + sp)
                e.wait_ge(s_yr, START + sp + 1)
                for c in range(ZC):
                    a = act(aff[:, c], tr[:, c // KC, (c % KC) * P:(c % KC + 1) * P], ACT.Identity,
                            bias=chan[:, 1, c:c + 1], scale=chan[:, 0, c:c + 1])
                a.then_inc(s_aff, 1)

            e.wait_ge(s_const, 16 * len(CONSTS))
            act(neg_a[:], neg_a[:], ACT.Exp).then_inc(s_expa, 1)
            with e.Fori(0, NB) as b:
                gb = e.snap(b * TILES)
                e.wait_ge(s_r0p, b + 1)
                e.wait_ge(s_zero, b + 1)
                act(cb[:, :, 1, 1:W + 1], tr[:, 0, 0:XC * W].rearrange("p (c w) -> p c w", w=W), ACT.Copy).then_inc(s_r0, 1)
                for c in range(ZC):
                    store_xbc(gb, c, False)
                e.wait_ge(s_lo, START + gb * SUBS)
                for n in range(TILES):
                    e.wait_ge(s_dtm, b * TILES + n + 1)
                    if n >= 4:
                        e.wait_ge(s_dtp, b * TILES + n - 3)
                    act(dt_rows(n), yp[0:HEADS, n % 2], ACT.Copy).then_inc(s_dtc, 1)
                store_xbc(gb, ZC, False)
                e.wait_ge(s_sp, b * SP_STEPS + 3)
                act(sp0[:], sp2, ACT.Exp).then_inc(s_dte, 1)
                for c in range(2):
                    silu(gb, 0, c)
                    store_xbc(e.snap(gb + 1), c, True)
                for n, (dst, src) in enumerate(((e_from, yp[:, 0]), (e_to, yp[:, 1]), (e_all, ring[0][:]))):
                    e.wait_ge(s_sum, b * 3 + n + 1)
                    act(dst[:], src[:, 0:NSUB * HEADS], ACT.Exp).then_inc(s_exps, 1)
                for i in range(SUBS):
                    e.wait_ge(s_out[i], START + gb * 16)
                e.wait_ge(s_first, (b + 1) * FIRST_STEPS)
                e.wait_ge(s_yoff, START + gb * SUBS * 2)
                for c in range(2, XC):
                    silu(gb, 0, c)

                def slot(t, u, i, first=False, top=False, left=TILES):
                    g = at_(e, gb + t)
                    s = e.snap(g * SUBS + i)
                    off, chunks = IN_PROJ[i]
                    chunks = chunks if off <= left else ()
                    if not first:
                        y_norm(e.snap(s - 1))
                    e.wait_ge(s_xtr, START + s + 1)
                    e.wait_ge(s_yi, START + s)
                    act(x_tok[:].rearrange("p (n c) -> p n c", n=2), tr[:, :, 0:HB], ACT.Copy).then_inc(s_xc, 1)
                    e.wait_ge(s_y, START + s)
                    for j in range(NG):
                        e.wait_ge(s_d, START + s * NG + j + 1)
                        act(mix[:, j], ring[j % 2][:], ACT.Exp).then_inc(s_e, 1)
                        if j == 0 and chunks:
                            store_xbc(e.snap(g + off), chunks[0], True)
                    if first:
                        e.wait_ge(s_zero, b + 1)
                    e.wait_ge(s_sa, START + s * 2)
                    e.wait_ge(s_yoff, START + s * 2)
                    for lo in (0, AT1, AT2):
                        a = act(state_st[lo:lo + NS], state[:], ACT.Copy)
                    a.then_inc(s_sh, 1)
                    if i % 2 == 0:
                        silu_z(g, i // 2, 0, g * 4 if i else e.snap(g * 4 - 2))
                    if not first:
                        y_scale(e.snap(s - 1))
                    if len(chunks) > 1:
                        store_xbc(e.snap(g + off), chunks[1], True)
                    if i % 2 == 0:
                        for q in range(1, 3):
                            silu_z(g, i // 2, q, g * 4 if i else e.snap(g * 4 - 2))
                    if left:
                        if i == 3:
                            e.wait_ge(s_yoff, START + g * SUBS * 2)
                        for c in range(2 * i, min(2 * i + 2, XC)):
                            silu(e.snap(g + 1), 1 - u, c)

                walk_scan(e, gb, slot)
                end = e.snap(gb + TILES)
                y_norm(e.snap(end * SUBS - 1))
                y_scale(e.snap(end * SUBS - 1))

                e.wait_ge(s_gr, b * 2 + 2)

                def l1_squares(q, i):
                    e.wait_ge(s_lt, START + q + 1)
                    act(xg_t[:, i % 2], pb[0][:, 0:C], ACT.Copy).then_inc(s_la, 1)
                    act(sq_t[:, i % 2], pb[0][:, 0:C], ACT.Square).then_inc(s_la, 1)

                def l1_boxes(q, i):
                    e.wait_ge(s_lw, q + 1)
                    act(s2[:, i % 2], tr[:, 0, 0:C], ACT.Square).then_inc(s_lb, 1)
                    act(qw[:, i % 2], tr[:, 1, 0:C], ACT.Copy).then_inc(s_lb, 1)

                def l1_x1(q, i):
                    e.wait_ge(s_lq, START + q + 1)
                    e.wait_ge(s_lo, START + q - 1)
                    act(x1_t[:, i % 2], pb[1][:, 0:C], ACT.Copy).then_inc(s_lr, 1)

                def l1_slot(t, u, i, stages=3, last=False):
                    g = at_(e, gb + t)
                    q = e.snap(g * SUBS + i)
                    l1_squares(q, i)
                    if stages > 1:
                        l1_boxes(e.snap(q - 1), (i - 1) % SUBS)
                    if stages > 2:
                        l1_x1(e.snap(q - 2), (i - 2) % SUBS)
                    if i == 1:
                        e.wait_ge(s_lq, START + g * SUBS)
                        at = e.snap(t * TT) if not isinstance(t, int) else t * TT
                        act(x1c, xb[:, :, bass.ds(at, TT)], ACT.Copy).then_inc(s_lc, 1)

                walk_layer1(e, l1_slot)
                l1_boxes(e.snap(end * SUBS - 1), SUBS - 1)
                for i in (SUBS - 2, SUBS - 1):
                    l1_x1(e.snap((end - 1) * SUBS + i), i)

        @block.vector
        def _(e):
            for counted in (s_lx, s_ls, s_sa, s_xtr, s_oev, s_g, s_yr):
                e.sem_inc(counted, START)
            def gn_steps(n, entries):
                at = n * GN_STEPS
                e.memset(g_red[:], 0.0)
                for k in range(KC):
                    e.bn_aggr(mean_var[:, k], stats[:, k, 0:entries].rearrange("p n s -> p (n s)")).then_inc(s_gv, 1)
                e.wait_ge(s_gp, n * 4 + 1)
                e.tensor_scalar(g_red[:, 0:1], yp[0:GROUPS, 0, 0:1], 1.0 / GC, None, ALU.mult).then_inc(s_gv, 1)
                e.wait_ge(s_gp, n * 4 + 2)
                e.tensor_copy(g_mean[:], yp[:, 1, 0:KC]).then_inc(s_gv, 1)
                e.wait_ge(s_gv, at + 5)
                e.tensor_tensor(g_tmp[:], mean_var[:, :, 0], g_mean[:], ALU.subtract).then_inc(s_gv, 1)
                e.wait_ge(s_gv, at + 6)
                e.tensor_tensor(g_tmp[:], g_tmp[:], g_tmp[:], ALU.mult).then_inc(s_gv, 1)
                e.wait_ge(s_gv, at + 7)
                e.tensor_tensor(g_tmp[:], g_tmp[:], mean_var[:, :, 1], ALU.add).then_inc(s_gv, 1)
                e.wait_ge(s_gp, n * 4 + 3)
                e.tensor_scalar(g_red[:, 1:2], yp[0:GROUPS, 0, 1:2], 1.0 / GC, None, ALU.mult).then_inc(s_gv, 1)
                e.wait_ge(s_gp, n * 4 + 4)
                e.tensor_scalar(g_var[:], yp[:, 1, KC:2 * KC], EPS, None, ALU.add).then_inc(s_gv, 1)

            def conv(gx, u, pair, lo, hi):
                at = gx * TPT + pair * TPP
                for n in range(lo, hi):
                    tap, side = n // 2, n % 2
                    if 2 * pair + 1 < XC:
                        c, r0, r1 = 2 * pair + side, 0, ROWS
                    else:
                        c, r0, r1 = 2 * pair, side * ROWS // 2, (side + 1) * ROWS // 2
                    dy, dx = tap // 3, tap % 3
                    src = cb[:, c, r0 + dy:r1 + dy, dx:dx + W]
                    acc = xs[:, u, c, r0 * W:r1 * W].rearrange("p (r w) -> p r w", w=W)
                    if tap == 0:
                        if side == 0 or 2 * pair + 1 < XC:
                            e.wait_ge(s_ev, START + (gx * XC + c + 1) * 2)
                        ins = e.tensor_scalar(acc, src, w_conv[:, c, 0:1], None, ALU.mult)
                    else:
                        e.wait_ge(s_tap, at + n - 1)
                        ins = e.scalar_tensor_tensor(out=acc, in0=src, scalar=w_conv[:, c, tap:tap + 1], in1=acc,
                                                     op0=ALU.mult, op1=ALU.add)
                    ins.then_inc(s_tap, 1)

            def gate_rows(sp, gx, i):
                h = i // 2
                e.wait_ge(s_aff, START + sp + 1)
                e.wait_ge(s_zev, START + gx * 6 + h * 3 + 3)
                v = gate[:, h, :, (i % 2) * P:(i % 2 + 1) * P]
                e.tensor_tensor(v, v, aff[:], ALU.mult).then_inc(s_g, 1)

            def add_out(gx, tx, h, q):
                e.wait_ge(s_op, START + gx * 4 + h * 2 + q + 1)
                e.wait_ge(s_res[h], gx * 16 + 16)
                ms = ((0, 1), (2,))[q]
                at = tx * TT + h * HALF
                at = e.snap(at) if not isinstance(at, int) else at
                for n, m in enumerate(ms):
                    ins = e.tensor_tensor(xb[:, m, bass.ds(at, HALF)], pb[1][:, n * HALF:(n + 1) * HALF],
                                          xres[:, h, m], ALU.add)
                ins.then_inc(s_oev, 1)
                e.wait_ge(s_oev, START + gx * 4 + h * 2 + q + 1)
                entry = tx * 2 + h
                entry = e.snap(entry) if not isinstance(entry, int) else entry
                for m in ms:
                    e.bn_stats(stats[:, m, bass.ds(entry, 1)].rearrange("p a s -> p (a s)"), xb[:, m, bass.ds(at, HALF)]).then_inc(s_x1st, 1)

            e.memset(cb[:], 0.0)
            e.memset(c_st[:].bitcast(F32), 0.0)
            e.memset(state_st[:].bitcast(F32), 0.0)
            e.memset(xb[:, :, H * W:(H + 1) * W], 0.0).then_inc(s_setup, 1)
            e.wait_ge(s_const, 16 * len(CONSTS))
            e.wait_ge(s_expa, 1)
            e.tensor_copy(after_r[:], after[:]).then_inc(s_setup, 1)
            e.tensor_scalar(neg_a[:], neg_a[:], -1.0, None, ALU.mult).then_inc(s_setup, 1)
            e.wait_ge(s_setup, 3)
            with e.Fori(0, NB) as b:
                gb = e.snap(b * TILES)
                e.wait_ge(s_yoff, START + gb * SUBS * 2)
                e.memset(cb[:, :, 0, :], 0.0)
                e.memset(state[:], 0.0).then_inc(s_zero, 1)
                e.wait_ge(s_x, (b + 1) * 16 * TILES)
                for t in range(TILES):
                    for k in range(KC):
                        e.bn_stats(stats[:, k, t], xb[:, k, t * TT:(t + 1) * TT]).then_inc(s_xst, 1)
                e.wait_ge(s_xst, (b + 1) * TILES * KC)
                n0 = e.snap(b * 2)
                gn_steps(n0, TILES)
                e.wait_ge(s_gr, n0 + 1)
                for lo, hi in ((0, 2 * TT), (2 * TT, H * W)):
                    for k in range(KC):
                        v = xb[:, k, lo:hi]
                        e.tensor_scalar(v, v, g_mean[:, k:k + 1], g_rstd[:, k:k + 1], ALU.subtract, ALU.mult
                                        ).then_inc(s_norm, 1)
                e.wait_ge(s_lo, START + gb * SUBS)
                e.wait_ge(s_r0, b + 1)
                for pair in range(PAIRS - 1):
                    if 2 * pair in FIRST_POOL:
                        e.wait_ge(s_tap, gb * TPT + pair * TPP)
                        e.sem_inc(s_tap, TPP)
                    else:
                        conv(gb, 0, pair, 0, TPP)
                at = e.snap(b * SP_STEPS)
                steps = [0]

                def step(ins):
                    steps[0] += 1
                    ins.then_inc(s_sp, 1)
                    e.wait_ge(s_sp, at + steps[0])

                def heads(v):
                    return v[:].unsqueeze(1).to_broadcast([P, NSUB, HEADS])

                def by_head(v):
                    return v[:].rearrange("p (n h) -> p n h", h=HEADS)

                e.wait_ge(s_dtp, (b + 1) * TILES)
                step(e.tensor_tensor(by_head(sp0), tr[:, 1, 0:NSUB * HEADS].rearrange("p (n h) -> p n h", h=HEADS),
                                     heads(dt_bias), ALU.add))
                step(e.tensor_scalar(sp1, sp0[:], 0.0, None, ALU.max))
                step(e.scalar_tensor_tensor(out=sp2, in0=sp1, scalar=-2.0, in1=sp0[:], op0=ALU.mult, op1=ALU.add))
                e.wait_ge(s_dte, b + 1)
                step(e.tensor_scalar(sp2, sp0[:], 2.0, None, ALU.add))
                step(e.reciprocal(sp2, sp2))
                step(e.tensor_tensor(sp0[:], sp0[:], sp2, ALU.mult))
                step(e.tensor_tensor(sp2, sp0[:], sp0[:], ALU.mult))
                step(e.tensor_scalar(dt[:], sp2, 1.0 / (2 * LOG_TERMS + 1), None, ALU.mult))
                for n in range(LOG_TERMS - 1, 0, -1):
                    step(e.scalar_tensor_tensor(out=dt[:], in0=dt[:], scalar=1.0 / (2 * n + 1), in1=sp2,
                                                op0=ALU.add, op1=ALU.mult))
                step(e.scalar_tensor_tensor(out=dt[:], in0=dt[:], scalar=1.0, in1=sp0[:], op0=ALU.add, op1=ALU.mult))
                step(e.scalar_tensor_tensor(out=dt[:], in0=dt[:], scalar=2.0, in1=sp1, op0=ALU.mult, op1=ALU.add))
                step(e.tensor_tensor(by_head(a_dt), by_head(dt), heads(neg_a), ALU.mult))
                step(e.tensor_copy(a_hi[:], a_dt))
                step(e.tensor_tensor(a_lo[:], a_dt, a_hi[:].bitcast(F32), ALU.subtract))
                assert steps[0] == SP_STEPS, steps

                conv(gb, 0, PAIRS - 1, 0, TPP)

                def slot(t, u, i, first=False, top=False, left=TILES):
                    g = at_(e, gb + t)
                    s = e.snap(g * SUBS + i)
                    at = e.snap((t * SUBS + i) * HEADS) if not isinstance(t, int) else (t * SUBS + i) * HEADS
                    cuts = CONV_CUTS[i]

                    def add_half(q):
                        if i == 3 and q == 0:
                            add_out(g, t, 0, q)
                        elif i == (1, 2)[q] and not top or i == 0 and q == 1 and not top:
                            before = t - 1 if isinstance(t, int) else e.snap(t - 1)
                            add_out(e.snap(g - 1), before, 1 if i else 0, q)

                    e.wait_ge(s_xt, s + 1)
                    e.tensor_copy(b_tok[:, i % 2], tr[:, 1, HB:HB + NS])
                    e.tensor_tensor(bc_m[:], tr[:, 0, HB:HB + P], upto[:], ALU.mult).then_inc(s_xtr, 1)
                    if left:
                        if i == 0:
                            e.wait_ge(s_y, START + g * SUBS)
                        g1 = e.snap(g + 1)
                        conv(g1, 1 - u, i, 0, cuts[0])
                    add_half(1)
                    if left:
                        conv(g1, 1 - u, i, cuts[0], cuts[1])
                    for j in range(NG):
                        if j == 0:
                            e.wait_ge(s_xtr, START + s + 1)
                        e.wait_ge(s_e, s * NG + j + 1)
                        v = mix[:, j].rearrange("p (h l) -> p h l", h=HG)
                        e.tensor_tensor(v, v, bc_m[:].unsqueeze(1).to_broadcast([P, HG, P]), ALU.mult).then_inc(s_m, 1)
                    if i == 0:
                        e.wait_ge(s_ch, g + 1)
                        e.wait_ge(s_yoff, START + s * 2)
                        e.tensor_tensor(c_st[AT2:STACK, u], ct[:, u], c_st[0:NS, u].bitcast(F32), ALU.subtract
                                        ).then_inc(s_cl, 1)
                    add_half(0)
                    if left:
                        conv(g1, 1 - u, i, cuts[1], cuts[2])
                    if not first:
                        gate_rows(e.snap(s - 1), g if i else e.snap(g - 1), (i - 1) % SUBS)
                    e.wait_ge(s_g, START + s)
                    for n in range(2):
                        e.wait_ge(s_yoff, START + s * 2 + n + 1)
                        e.tensor_tensor(y_in[:, n * HB:(n + 1) * HB].rearrange("p (h d) -> p h d", d=HD),
                                        ring[1 - n][:, 0:HB].rearrange("p (h d) -> p h d", d=HD),
                                        e_from[:, bass.ds(at + n * HEADS // 2, HEADS // 2)].unsqueeze(2)
                                        .to_broadcast([P, HEADS // 2, HD]), ALU.mult).then_inc(s_t1, 1)
                    if left:
                        conv(g1, 1 - u, i, cuts[2], cuts[3])
                    e.wait_ge(s_yi, START + s + 1)
                    e.wait_ge(s_ynt, START + s)
                    e.tensor_tensor(y[:].rearrange("p (n c) -> p n c", n=2), yp[:, :, 0:HB],
                                    y_in.rearrange("p (n c) -> p n c", n=2), ALU.add).then_inc(s_yr, 1)
                    e.wait_ge(s_yr, START + s + 1)
                    for n in range(2):
                        e.bn_stats(ln_st[:, n], y[:, n * HB:(n + 1) * HB]).then_inc(s_yst, 1)
                    e.wait_ge(s_yst, s * 3 + 2)
                    e.memset(g_red[:], 0.0)
                    e.bn_aggr(ln_mv[:], ln_st[:].rearrange("p n s -> p (n s)")).then_inc(s_yst, 1)
                    e.wait_ge(s_yst, s * 3 + 3)
                    e.wait_ge(s_rs, START + s * 2)
                    e.tensor_scalar(ln_vm[:, 1:2], ln_mv[:, 0:1], -1.0, None, ALU.mult)
                    e.tensor_scalar(ln_vm[:, 0:1], ln_mv[:, 1:2], EPS, None, ALU.add).then_inc(s_var, 1)
                    e.wait_ge(s_ss, s + 1)
                    for n in range(2):
                        e.wait_ge(s_sn, START + s * 2 + n + 1)
                        v = state[:, n * HB:(n + 1) * HB]
                        e.tensor_tensor(v, ring[1 - n][0:NS, 0:HB], v, ALU.add).then_inc(s_sa, 1)

                walk_scan(e, gb, slot)
                end = e.snap(gb + TILES)
                last = e.snap(end - 1)
                gate_rows(e.snap(end * SUBS - 1), last, SUBS - 1)
                add_out(last, TILES - 1, 0, 1)
                for q in range(2):
                    add_out(last, TILES - 1, 1, q)

                e.wait_ge(s_x1st, end * 2 * KC)
                n1 = e.snap(b * 2 + 1)
                gn_steps(n1, 2 * TILES)
                e.wait_ge(s_gr, n1 + 1)

                def l1_norm(t, u):
                    at = e.snap(t * TT) if not isinstance(t, int) else t * TT
                    for k in range(KC):
                        ins = e.tensor_scalar(xg[u][:, k], xb[:, k, bass.ds(at, TT)], g_mean[:, k:k + 1], g_rstd[:, k:k + 1],
                                              ALU.subtract, ALU.mult)
                    ins.then_inc(s_lx, 1)

                def l1_ratio(q, i):
                    e.wait_ge(s_lq, START + q + 1)
                    e.wait_ge(s_lo, START + q - 1)
                    e.tensor_scalar(den[:, i % 2], l1_den(i)[:, 0:C], TINY, None, ALU.max).then_inc(s_ls, 1)
                    e.wait_ge(s_ls, START + q * 3 + 1)
                    e.reciprocal(rec, den[:, i % 2]).then_inc(s_ls, 1)
                    e.wait_ge(s_ls, START + q * 3 + 2)
                    e.tensor_tensor(ratio[:, i % 2], l1_num(i)[:, 0:C], rec, ALU.mult).then_inc(s_ls, 1)

                l1_norm(0, 0)

                def l1_slot(t, u, i, stages=3, last=False):
                    g = at_(e, gb + t)
                    if stages > 2:
                        l1_ratio(e.snap(g * SUBS + i - 2), (i - 2) % SUBS)
                    if i == 1 and not last:
                        e.wait_ge(s_lt, START + g * SUBS)
                        l1_norm(t + 1, 1 - u)

                walk_layer1(e, l1_slot)
                l1_ratio(e.snap(end * SUBS - 2), SUBS - 2)
                l1_ratio(e.snap(end * SUBS - 1), SUBS - 1)


def layout(x, w_in, w_conv, b_conv, dt_bias, a_log, d_param, gamma, beta, w_out):
    f = np.float32

    def by_partition(a, k):
        return np.ascontiguousarray(np.moveaxis(a.reshape(k, P, *a.shape[1:]), 0, 1))

    xbc = np.zeros((C, XC * P), f)
    xbc[:, 0:DI + NS] = w_in[:, DI:2 * DI + NS]
    xbc[:, DI + C_AT:DI + C_AT + NS] = w_in[:, 2 * DI + NS:2 * DI + 2 * NS]
    wc, bc = np.zeros((XC * P, TAPS), f), np.zeros((XC * P,), f)
    taps = w_conv.reshape(TAPS, -1).T
    wc[0:DI + NS], bc[0:DI + NS] = taps[0:DI + NS], b_conv[0:DI + NS]
    at = DI + C_AT
    wc[at:at + NS], bc[at:at + NS] = taps[DI + NS:], b_conv[DI + NS:]
    chan = np.stack([gamma.reshape(ZC, P), beta.reshape(ZC, P)])
    k, m = np.arange(P)[:, None], np.arange(P)[None, :]
    ch, grp = np.arange(C), np.arange(GROUPS)
    to_group = (ch[:, None] // GC == grp[None, :]).astype(f)
    lo, hi = WIN_W // 2, WIN_W - WIN_W // 2 - 1
    band_w = ((k // W == m // W) & (k >= m - lo) & (k <= m + hi)).astype(f)
    count = band_w.sum(0, keepdims=True)
    lo, hi = WIN_C // 2, WIN_C - WIN_C // 2 - 1
    band = ((ch[:, None] >= ch[None, :] - lo) & (ch[:, None] <= ch[None, :] + hi)).astype(f)
    band_c = np.zeros((P, KC, BANDC), f)
    for n in range(KC):
        band_c[:, n, 0:BAND_HI[n] - BAND_LO[n]] = band[n * P:(n + 1) * P, BAND_LO[n]:BAND_HI[n]]
    xt = x.reshape(NB * TILES, TT, KC, P).transpose(0, 3, 2, 1)
    return {
        "x": np.ascontiguousarray(xt),
        "w_xbc": by_partition(xbc, KC), "w_z": by_partition(w_in[:, 0:DI], KC),
        "w_dt": by_partition(w_in[:, 2 * DI + 2 * NS:], KC), "w_out": by_partition(w_out, ZC),
        "w_conv": by_partition(wc, XC), "b_conv": by_partition(bc, XC),
        "chan": np.ascontiguousarray(chan.transpose(2, 0, 1)),
        "d_heads": np.tile(d_param, (P, 1)), "dt_bias": np.tile(dt_bias, (P, 1)), "neg_a": np.tile(a_log, (P, 1)),
        "upto": (k <= m).astype(f), "after": (k > m).astype(f), "ones": np.ones((P, P), f),
        "ident": np.eye(P, dtype=f), "to_group": by_partition(to_group, KC),
        "from_group": np.ascontiguousarray(to_group.T), "band_w": band_w, "band_wn": band_w * count, "band_c": band_c,
    }


def kernel(x, L0_conv_W_in, L0_conv_W_conv, L0_conv_b_conv, L0_conv_dt_bias, L0_conv_A_log, L0_conv_D_param,
           L0_conv_gamma, L0_conv_beta, L0_conv_W_out):
    import concourse.bacc as bacc
    from concourse.bass_utils import run_bass_kernel_spmd

    arrays = layout(*(np.asarray(v) for v in (
        x, L0_conv_W_in, L0_conv_W_conv, L0_conv_b_conv, L0_conv_dt_bias, L0_conv_A_log, L0_conv_D_param,
        L0_conv_gamma, L0_conv_beta, L0_conv_W_out)))
    nc = bacc.Bacc("TRN2", target_bir_lowering=False, num_devices=1)
    aps = {n: nc.dram_tensor(f"in_{n}", a.shape, mybir.dt.from_np(a.dtype), kind="ExternalInput").ap()
           for n, a in arrays.items()}
    aps["out"] = nc.dram_tensor("out", (NB * TILES, TT, C), F32, kind="ExternalOutput").ap()
    build(nc, aps)
    r = run_bass_kernel_spmd(nc, [{f"in_{n}": a for n, a in arrays.items()}], core_ids=[0])
    return r.results[0]["out"].reshape(NB, H, W, C)
```
